# Optimizing a Trainium2 kernel written in Bass

```python
import numpy as np
import jax
import jax.numpy as jnp

def _softmax(x, axis=-1):
    return jax.nn.softmax(x, axis=axis)

def _gelu(x):
    return jax.nn.gelu(x, approximate=True)

def _silu(x):
    return jax.nn.silu(x)

def _sigmoid(x):
    return jax.nn.sigmoid(x)

def _layernorm(x, axis=-1, eps=1e-05):
    m = jnp.mean(x, axis=axis, keepdims=True)
    v = jnp.var(x, axis=axis, keepdims=True)
    return (x - m) / jnp.sqrt(v + eps)

def _scatter_add(tgt, idx, src, axis=0):
    return tgt.at[idx].add(src)

def _segment_sum(src, seg, n):
    return jax.ops.segment_sum(src, seg, n)
kernel_name = 'mk_gnn_preln_d4_gnn_r16_ba088c'

def setup_inputs(seed: int=0):
    np.random.seed(seed)
    _w = jnp.asarray

    def _rec_inputs():
        import jax
        import jax.numpy as jnp
        _gk = jax.random.key(seed)
        x = -0.000202 + 1 * jax.random.normal(jax.random.fold_in(_gk, 1), (6250, 128), jnp.float32)
        src = jax.random.randint(jax.random.fold_in(_gk, 2), (200000,), 0, 6250, jnp.int32)
        dst = jnp.minimum((6250 * jax.random.uniform(jax.random.fold_in(_gk, 3), (200000,)) ** 2.0).astype(jnp.int32), 99999)
        _o = jnp.argsort(dst, stable=True)
        src = src[_o]
        dst = dst[_o]
        edge_attr_64 = 0.000155561 + 1.00019 * jax.random.normal(jax.random.fold_in(_gk, 11), (200000, 64), jnp.float32)
        edge_attr_9 = 0.000458729 + 1.00015 * jax.random.normal(jax.random.fold_in(_gk, 12), (200000, 9), jnp.float32)
        return (x, src, dst, edge_attr_64, edge_attr_9)
    x, src, dst, edge_attr_64, edge_attr_9 = _rec_inputs()

    def _L0_gnn_setup():
        import jax, jax.numpy as jnp
        import numpy as np
        N_NODES = 3125
        D_FEAT = 128
        N_EDGES = 37500
        ALPHA = 0.1

        def _appnp_k1(x, edge_index):
            n = x.shape[0]
            loops = jnp.arange(n, dtype=edge_index.dtype)
            src = jnp.concatenate([edge_index[0], loops])
            dst = jnp.concatenate([edge_index[1], loops])
            ones = jnp.ones(src.shape[0], dtype=x.dtype)
            deg = jax.ops.segment_sum(ones, dst, num_segments=n)
            dinv = jnp.where(deg > 0, jax.lax.rsqrt(deg), 0.0)
            norm = dinv[src] * dinv[dst]
            agg = jax.ops.segment_sum(x[src] * norm[:, None], dst, num_segments=n)
            return (1.0 - ALPHA) * agg + ALPHA * x
        key = jax.random.key(seed)
        k1, k2 = jax.random.split(key)
        x = jax.random.normal(k1, (N_NODES, D_FEAT), dtype=jnp.float32)
        edge_index = jax.random.randint(k2, (2, N_EDGES), 0, N_NODES, dtype=jnp.int64)
        return {'x': x, 'edge_index': edge_index}
    _L0_gnn_all = _L0_gnn_setup()
    _L0_gnn_in = {k: v for k, v in _L0_gnn_all.items() if k in ()}
    del _L0_gnn_all

    def _L1_gnn_setup():
        import jax, jax.numpy as jnp
        import numpy as np
        from fractions import Fraction
        from math import factorial

        def _su2_cg_coeff(j1, m1, j2, m2, j3, m3):
            if m3 != m1 + m2:
                return 0.0
            vmin = int(max(-j1 + j2 + m3, -j1 + m1, 0))
            vmax = int(min(j2 + j3 + m1, j3 - j1 + j2, j3 + m3))
            f = lambda n: factorial(round(n))
            C = ((2.0 * j3 + 1.0) * Fraction(f(j3 + j1 - j2) * f(j3 - j1 + j2) * f(j1 + j2 - j3) * f(j3 + m3) * f(j3 - m3), f(j1 + j2 + j3 + 1) * f(j1 - m1) * f(j1 + m1) * f(j2 - m2) * f(j2 + m2))) ** 0.5
            S = 0
            for v in range(vmin, vmax + 1):
                S += (-1) ** (v + j2 + m2) * Fraction(f(j2 + j3 + m1 - v) * f(j1 - m1 + v), f(v) * f(j3 - j1 + j2 - v) * f(j3 + m3 - v) * f(v + j1 - j2 - m3))
            return float(C * S)

        def _change_basis_real_to_complex(l):
            q = np.zeros((2 * l + 1, 2 * l + 1), dtype=np.complex128)
            for m in range(-l, 0):
                q[l + m, l + abs(m)] = 1 / np.sqrt(2)
                q[l + m, l - abs(m)] = -1j / np.sqrt(2)
            q[l, l] = 1
            for m in range(1, l + 1):
                q[l + m, l + abs(m)] = (-1) ** m / np.sqrt(2)
                q[l + m, l - abs(m)] = 1j * (-1) ** m / np.sqrt(2)
            return (-1j) ** l * q

        def wigner_3j(l1, l2, l3):
            C = np.zeros((2 * l1 + 1, 2 * l2 + 1, 2 * l3 + 1))
            for m1 in range(-l1, l1 + 1):
                for m2 in range(-l2, l2 + 1):
                    m3 = m1 + m2
                    if abs(m3) <= l3:
                        C[l1 + m1, l2 + m2, l3 + m3] = _su2_cg_coeff(l1, m1, l2, m2, l3, m3)
            Q1 = _change_basis_real_to_complex(l1)
            Q2 = _change_basis_real_to_complex(l2)
            Q3 = _change_basis_real_to_complex(l3)
            Cc = np.einsum('ij,kl,mn,ikn->jlm', Q1, Q2, np.conj(Q3.T), C.astype(np.complex128))
            Cr = np.real(Cc)
            return Cr / np.linalg.norm(Cr)
        MUL = 32
        IRREPS_IN = [(MUL, 0, 1), (MUL, 1, -1)]
        IRREPS_SH = [(1, 0, 1), (1, 1, -1), (1, 2, 1)]
        IRREPS_OUT = [(MUL, 0, 1), (MUL, 1, -1)]
        NUM_NEIGHBORS = 10.0
        N_NODES, N_EDGES = (625, 6250)

        def _dim(irreps):
            return sum((m * (2 * l + 1) for m, l, _ in irreps))

        def _slices(irreps):
            s, out = (0, [])
            for m, l, _ in irreps:
                d = m * (2 * l + 1)
                out.append((s, s + d))
                s += d
            return out

        def _instructions():
            ins = []
            for i1, (m1, l1, p1) in enumerate(IRREPS_IN):
                for i2, (m2, l2, p2) in enumerate(IRREPS_SH):
                    for io, (mo, lo, po) in enumerate(IRREPS_OUT):
                        if abs(l1 - l2) <= lo <= l1 + l2 and p1 * p2 == po:
                            ins.append((i1, i2, io))
            return ins
        _INSTR = _instructions()
        _SL_IN, _SL_SH, _SL_OUT = (_slices(IRREPS_IN), _slices(IRREPS_SH), _slices(IRREPS_OUT))
        _W3J = [jnp.asarray(wigner_3j(IRREPS_IN[i1][1], IRREPS_SH[i2][1], IRREPS_OUT[io][1]), dtype=jnp.float32) for i1, i2, io in _INSTR]
        _NORM = []
        for _i1, _i2, _io in _INSTR:
            _alpha = 2 * IRREPS_OUT[_io][1] + 1
            _x = sum((IRREPS_IN[j1][0] * IRREPS_SH[j2][0] for j1, j2, jo in _INSTR if jo == _io))
            _NORM.append(float(np.sqrt(_alpha / _x)))

        def _tensor_product(x1, x2, weights):
            E = x1.shape[0]
            out = jnp.zeros((E, _dim(IRREPS_OUT)), dtype=x1.dtype)
            for k, (i1, i2, io) in enumerate(_INSTR):
                m1, l1, _ = IRREPS_IN[i1]
                m2, l2, _ = IRREPS_SH[i2]
                mo, lo, _ = IRREPS_OUT[io]
                a, b = _SL_IN[i1]
                c, d = _SL_SH[i2]
                e, f = _SL_OUT[io]
                x1s = x1[:, a:b].reshape(E, m1, 2 * l1 + 1)
                x2s = x2[:, c:d].reshape(E, m2, 2 * l2 + 1)
                seg = jnp.einsum('uvw,ijk,eui,evj->ewk', weights[k], _W3J[k], x1s, x2s, optimize='optimal') * _NORM[k]
                out = out.at[:, e:f].add(seg.reshape(E, mo * (2 * lo + 1)))
            return out
        key = jax.random.key(seed)
        ks = jax.random.split(key, 8)
        x = jax.random.normal(ks[0], (N_NODES, _dim(IRREPS_IN)), dtype=jnp.float32)
        edge_index = jax.random.randint(ks[1], (2, N_EDGES), 0, N_NODES)
        edge_attr = jax.random.normal(ks[2], (N_EDGES, _dim(IRREPS_SH)), dtype=jnp.float32)
        ws = {f'w{k}': jax.random.normal(ks[3 + k], (MUL, 1, MUL), dtype=jnp.float32) for k in range(len(_INSTR))}
        return {'x': x, 'edge_index': edge_index, 'edge_attr': edge_attr, **ws}
    _L1_gnn_all = _L1_gnn_setup()
    _L1_gnn_in = {k: v for k, v in _L1_gnn_all.items() if k in ('w0', 'w1', 'w2', 'w3', 'w4')}
    del _L1_gnn_all

    def _L2_gnn_setup():
        import jax, jax.numpy as jnp
        import numpy as np
        N_NODES, N_EDGES = (3125, 37500)
        NODE_DIM, EDGE_DIM = (128, 64)
        H, HD = (4, 32)
        key = jax.random.key(seed)
        k = jax.random.split(key, 6)
        node_features = jax.random.normal(k[0], (N_NODES, NODE_DIM), jnp.float32)
        edge_indices = jax.random.randint(k[1], (2, N_EDGES), 0, N_NODES, jnp.int32)
        edge_features = jax.random.normal(k[2], (N_EDGES, EDGE_DIM), jnp.float32)
        W_node = jax.random.normal(k[3], (H * HD, NODE_DIM), jnp.float32) / np.sqrt(NODE_DIM).astype(np.float32)
        W_edge = jax.random.normal(k[4], (H * HD, EDGE_DIM), jnp.float32) / np.sqrt(EDGE_DIM).astype(np.float32)
        a = jax.random.normal(k[5], (H, 3 * HD), jnp.float32)
        return {'node_features': node_features, 'edge_indices': edge_indices, 'edge_features': edge_features, 'W_node': W_node, 'W_edge': W_edge, 'a': a}
    _L2_gnn_all = _L2_gnn_setup()
    _L2_gnn_in = {k: v for k, v in _L2_gnn_all.items() if k in ('W_node', 'W_edge', 'a')}
    del _L2_gnn_all

    def _L3_gnn_setup():
        import jax, jax.numpy as jnp
        import numpy as np
        N_NODES = 6250
        N_EDGES = 50000
        D_IN = 128
        D_OUT = 128
        LN_EPS = 1e-05
        key = jax.random.key(seed)
        ks = jax.random.split(key, 8)
        node_features = jax.random.normal(ks[0], (N_NODES, D_IN), dtype=jnp.float32)
        edge_index = jax.random.randint(ks[1], (2, N_EDGES), 0, N_NODES, dtype=jnp.int64)
        s = 1.0 / np.sqrt(D_IN)
        W_self = jax.random.uniform(ks[2], (D_IN, D_OUT), minval=-s, maxval=s, dtype=jnp.float32)
        b_self = jax.random.uniform(ks[3], (D_OUT,), minval=-s, maxval=s, dtype=jnp.float32)
        W_msg = jax.random.uniform(ks[4], (D_IN, D_OUT), minval=-s, maxval=s, dtype=jnp.float32)
        b_msg = jax.random.uniform(ks[5], (D_OUT,), minval=-s, maxval=s, dtype=jnp.float32)
        ln_gamma = jnp.ones((D_OUT,), dtype=jnp.float32)
        ln_beta = jnp.zeros((D_OUT,), dtype=jnp.float32)
        return {'node_features': node_features, 'edge_index': edge_index, 'W_self': W_self, 'b_self': b_self, 'W_msg': W_msg, 'b_msg': b_msg, 'ln_gamma': ln_gamma, 'ln_beta': ln_beta}
    _L3_gnn_all = _L3_gnn_setup()
    _L3_gnn_in = {k: v for k, v in _L3_gnn_all.items() if k in ('W_self', 'b_self', 'W_msg', 'b_msg', 'ln_gamma', 'ln_beta')}
    del _L3_gnn_all
    return {'x': x, 'src': src, 'dst': dst, 'edge_attr_64': edge_attr_64, 'edge_attr_9': edge_attr_9, 'L1_gnn_w0': _L1_gnn_in['w0'], 'L1_gnn_w1': _L1_gnn_in['w1'], 'L1_gnn_w2': _L1_gnn_in['w2'], 'L1_gnn_w3': _L1_gnn_in['w3'], 'L1_gnn_w4': _L1_gnn_in['w4'], 'L2_gnn_W_node': _L2_gnn_in['W_node'], 'L2_gnn_W_edge': _L2_gnn_in['W_edge'], 'L2_gnn_a': _L2_gnn_in['a'], 'L3_gnn_W_self': _L3_gnn_in['W_self'], 'L3_gnn_b_self': _L3_gnn_in['b_self'], 'L3_gnn_W_msg': _L3_gnn_in['W_msg'], 'L3_gnn_b_msg': _L3_gnn_in['b_msg'], 'L3_gnn_ln_gamma': _L3_gnn_in['ln_gamma'], 'L3_gnn_ln_beta': _L3_gnn_in['ln_beta']}

def reference(x, src, dst, edge_attr_64, edge_attr_9, L1_gnn_w0, L1_gnn_w1, L1_gnn_w2, L1_gnn_w3, L1_gnn_w4, L2_gnn_W_node, L2_gnn_W_edge, L2_gnn_a, L3_gnn_W_self, L3_gnn_b_self, L3_gnn_W_msg, L3_gnn_b_msg, L3_gnn_ln_gamma, L3_gnn_ln_beta):
    import jax
    import jax.numpy as jnp

    def _L0_gnn_ref(x, edge_index):
        import jax, jax.numpy as jnp
        import numpy as np
        N_NODES = 3125
        D_FEAT = 128
        N_EDGES = 37500
        ALPHA = 0.1

        def _appnp_k1(x, edge_index):
            n = x.shape[0]
            loops = jnp.arange(n, dtype=edge_index.dtype)
            src = jnp.concatenate([edge_index[0], loops])
            dst = jnp.concatenate([edge_index[1], loops])
            ones = jnp.ones(src.shape[0], dtype=x.dtype)
            deg = jax.ops.segment_sum(ones, dst, num_segments=n)
            dinv = jnp.where(deg > 0, jax.lax.rsqrt(deg), 0.0)
            norm = dinv[src] * dinv[dst]
            agg = jax.ops.segment_sum(x[src] * norm[:, None], dst, num_segments=n)
            return (1.0 - ALPHA) * agg + ALPHA * x
        h = _appnp_k1(x, edge_index)
        return x + jax.nn.relu(h)

    def _L1_gnn_ref(x, edge_index, edge_attr, w0, w1, w2, w3, w4):
        import jax, jax.numpy as jnp
        import numpy as np
        from fractions import Fraction
        from math import factorial

        def _su2_cg_coeff(j1, m1, j2, m2, j3, m3):
            if m3 != m1 + m2:
                return 0.0
            vmin = int(max(-j1 + j2 + m3, -j1 + m1, 0))
            vmax = int(min(j2 + j3 + m1, j3 - j1 + j2, j3 + m3))
            f = lambda n: factorial(round(n))
            C = ((2.0 * j3 + 1.0) * Fraction(f(j3 + j1 - j2) * f(j3 - j1 + j2) * f(j1 + j2 - j3) * f(j3 + m3) * f(j3 - m3), f(j1 + j2 + j3 + 1) * f(j1 - m1) * f(j1 + m1) * f(j2 - m2) * f(j2 + m2))) ** 0.5
            S = 0
            for v in range(vmin, vmax + 1):
                S += (-1) ** (v + j2 + m2) * Fraction(f(j2 + j3 + m1 - v) * f(j1 - m1 + v), f(v) * f(j3 - j1 + j2 - v) * f(j3 + m3 - v) * f(v + j1 - j2 - m3))
            return float(C * S)

        def _change_basis_real_to_complex(l):
            q = np.zeros((2 * l + 1, 2 * l + 1), dtype=np.complex128)
            for m in range(-l, 0):
                q[l + m, l + abs(m)] = 1 / np.sqrt(2)
                q[l + m, l - abs(m)] = -1j / np.sqrt(2)
            q[l, l] = 1
            for m in range(1, l + 1):
                q[l + m, l + abs(m)] = (-1) ** m / np.sqrt(2)
                q[l + m, l - abs(m)] = 1j * (-1) ** m / np.sqrt(2)
            return (-1j) ** l * q

        def wigner_3j(l1, l2, l3):
            C = np.zeros((2 * l1 + 1, 2 * l2 + 1, 2 * l3 + 1))
            for m1 in range(-l1, l1 + 1):
                for m2 in range(-l2, l2 + 1):
                    m3 = m1 + m2
                    if abs(m3) <= l3:
                        C[l1 + m1, l2 + m2, l3 + m3] = _su2_cg_coeff(l1, m1, l2, m2, l3, m3)
            Q1 = _change_basis_real_to_complex(l1)
            Q2 = _change_basis_real_to_complex(l2)
            Q3 = _change_basis_real_to_complex(l3)
            Cc = np.einsum('ij,kl,mn,ikn->jlm', Q1, Q2, np.conj(Q3.T), C.astype(np.complex128))
            Cr = np.real(Cc)
            return Cr / np.linalg.norm(Cr)
        MUL = 32
        IRREPS_IN = [(MUL, 0, 1), (MUL, 1, -1)]
        IRREPS_SH = [(1, 0, 1), (1, 1, -1), (1, 2, 1)]
        IRREPS_OUT = [(MUL, 0, 1), (MUL, 1, -1)]
        NUM_NEIGHBORS = 10.0
        N_NODES, N_EDGES = (625, 6250)

        def _dim(irreps):
            return sum((m * (2 * l + 1) for m, l, _ in irreps))

        def _slices(irreps):
            s, out = (0, [])
            for m, l, _ in irreps:
                d = m * (2 * l + 1)
                out.append((s, s + d))
                s += d
            return out

        def _instructions():
            ins = []
            for i1, (m1, l1, p1) in enumerate(IRREPS_IN):
                for i2, (m2, l2, p2) in enumerate(IRREPS_SH):
                    for io, (mo, lo, po) in enumerate(IRREPS_OUT):
                        if abs(l1 - l2) <= lo <= l1 + l2 and p1 * p2 == po:
                            ins.append((i1, i2, io))
            return ins
        _INSTR = _instructions()
        _SL_IN, _SL_SH, _SL_OUT = (_slices(IRREPS_IN), _slices(IRREPS_SH), _slices(IRREPS_OUT))
        _W3J = [jnp.asarray(wigner_3j(IRREPS_IN[i1][1], IRREPS_SH[i2][1], IRREPS_OUT[io][1]), dtype=jnp.float32) for i1, i2, io in _INSTR]
        _NORM = []
        for _i1, _i2, _io in _INSTR:
            _alpha = 2 * IRREPS_OUT[_io][1] + 1
            _x = sum((IRREPS_IN[j1][0] * IRREPS_SH[j2][0] for j1, j2, jo in _INSTR if jo == _io))
            _NORM.append(float(np.sqrt(_alpha / _x)))

        def _tensor_product(x1, x2, weights):
            E = x1.shape[0]
            out = jnp.zeros((E, _dim(IRREPS_OUT)), dtype=x1.dtype)
            for k, (i1, i2, io) in enumerate(_INSTR):
                m1, l1, _ = IRREPS_IN[i1]
                m2, l2, _ = IRREPS_SH[i2]
                mo, lo, _ = IRREPS_OUT[io]
                a, b = _SL_IN[i1]
                c, d = _SL_SH[i2]
                e, f = _SL_OUT[io]
                x1s = x1[:, a:b].reshape(E, m1, 2 * l1 + 1)
                x2s = x2[:, c:d].reshape(E, m2, 2 * l2 + 1)
                seg = jnp.einsum('uvw,ijk,eui,evj->ewk', weights[k], _W3J[k], x1s, x2s, optimize='optimal') * _NORM[k]
                out = out.at[:, e:f].add(seg.reshape(E, mo * (2 * lo + 1)))
            return out
        i, j = (edge_index[0], edge_index[1])
        summand = _tensor_product(x[i], edge_attr, [w0, w1, w2, w3, w4])
        out = jax.ops.segment_sum(summand, j, num_segments=x.shape[0])
        return out / float(np.sqrt(NUM_NEIGHBORS))

    def _L2_gnn_ref(node_features, edge_indices, edge_features, W_node, W_edge, a):
        import jax, jax.numpy as jnp
        import numpy as np
        N_NODES, N_EDGES = (3125, 37500)
        NODE_DIM, EDGE_DIM = (128, 64)
        H, HD = (4, 32)
        num_nodes = node_features.shape[0]
        num_edges = edge_indices.shape[1]
        h = (node_features @ W_node.T).reshape(num_nodes, H, HD)
        e = (edge_features @ W_edge.T).reshape(num_edges, H, HD)
        src, tgt = (edge_indices[0], edge_indices[1])
        h_src = h[src]
        h_tgt = h[tgt]
        att_in = jnp.concatenate([h_src, h_tgt, e], axis=-1)
        att = jnp.sum(att_in * a, axis=-1)
        att = jnp.where(att > 0, att, 0.2 * att)
        m = jnp.maximum(jax.ops.segment_max(att, tgt, num_segments=num_nodes), 0.0)
        ex = jnp.exp(att - m[tgt])
        ones = jnp.ones((num_edges,), node_features.dtype)
        deg = jax.ops.segment_sum(ones, tgt, num_segments=num_nodes)
        denom = jax.ops.segment_sum(ex, tgt, num_segments=num_nodes) + (num_edges - deg)[:, None] * jnp.exp(-m)
        w = ex / denom[tgt]
        h_prime = jax.ops.segment_sum(w[:, :, None] * h_src, tgt, num_segments=num_nodes)
        return h_prime.reshape(num_nodes, H * HD)

    def _L3_gnn_ref(node_features, edge_index, W_self, b_self, W_msg, b_msg, ln_gamma, ln_beta):
        import jax, jax.numpy as jnp
        import numpy as np
        N_NODES = 6250
        N_EDGES = 50000
        D_IN = 128
        D_OUT = 128
        LN_EPS = 1e-05
        num_nodes = node_features.shape[0]
        src = edge_index[0]
        tgt = edge_index[1]
        messages = node_features[src] @ W_msg + b_msg
        agg = jax.ops.segment_sum(messages, tgt, num_segments=num_nodes)
        degree = jax.ops.segment_sum(jnp.ones((src.shape[0],), dtype=node_features.dtype), tgt, num_segments=num_nodes)
        agg = agg / jnp.maximum(degree, 1.0)[:, None]
        combined = node_features @ W_self + b_self + agg
        mean = jnp.mean(combined, axis=-1, keepdims=True)
        var = jnp.var(combined, axis=-1, keepdims=True)
        normed = (combined - mean) * jax.lax.rsqrt(var + LN_EPS) * ln_gamma + ln_beta
        return jax.nn.relu(normed)
    edge_index = jnp.stack([src, dst])
    h = jnp.maximum(_layernorm(x, axis=-1), 0.0)
    x = x + _L0_gnn_ref(h, edge_index)
    h = jnp.maximum(_layernorm(x, axis=-1), 0.0)
    x = x + _L1_gnn_ref(h, edge_index, edge_attr_9, L1_gnn_w0, L1_gnn_w1, L1_gnn_w2, L1_gnn_w3, L1_gnn_w4)
    h = jnp.maximum(_layernorm(x, axis=-1), 0.0)
    x = x + _L2_gnn_ref(h, edge_index, edge_attr_64, L2_gnn_W_node, L2_gnn_W_edge, L2_gnn_a)
    h = jnp.maximum(_layernorm(x, axis=-1), 0.0)
    x = x + _L3_gnn_ref(h, edge_index, L3_gnn_W_self, L3_gnn_b_self, L3_gnn_W_msg, L3_gnn_b_msg, L3_gnn_ln_gamma, L3_gnn_ln_beta)
    return x

_drawn_inputs = setup_inputs


def setup_inputs(seed=0):
    import zlib

    import numpy as np

    out = dict(_drawn_inputs(seed))
    spreads = {'L3_gnn_ln_gamma': (1.0, 0.2), 'L3_gnn_ln_beta': (0.0, 0.307)}
    factors = {}
    for name, (base, spread) in spreads.items():
        noise = np.random.default_rng([zlib.crc32(name.encode()), seed]).standard_normal(out[name].shape)
        drawn = base * np.exp(spread * noise) if base else spread * noise
        out[name] = jnp.asarray(drawn.astype(out[name].dtype))
    for name, factor in factors.items():
        out[name] = (out[name] * factor).astype(out[name].dtype)
    return out
```

```python
from contextlib import ExitStack

import numpy as np
import concourse.bass as bass
from concourse import mybir

F32 = mybir.dt.float32
BF16 = mybir.dt.bfloat16
I32 = mybir.dt.int32
ALU = mybir.AluOpType
ACT = mybir.ActivationFunctionType
AX = mybir.AxisListType

P = 128
D = 128
J = 8
GROUP = P * J
U = 4
WIN = 128
NB = 7
EPS = 1e-5
FAR = -1.0e6
DMA = 16


def ds(start, size):
    return bass.ds(start, size)


class Shapes:

    def __init__(self, n_nodes, n_edges):
        self.n = n_nodes
        self.e = n_edges
        self.groups = -(-n_edges // GROUP)
        assert self.groups % U == 0 and n_edges % J == 0
        self.rounds = self.groups // U
        self.blocks = -(-n_nodes // P)
        assert self.blocks % NB == 0
        self.node_rounds = self.blocks // NB
        self.rows = self.blocks * P
        self.cols = self.rows + WIN
        self.overlap = self.groups * GROUP - n_edges
        self.last_block = n_nodes - (self.blocks - 1) * P

    def first_edge(self, rnd, u):
        start = rnd * (U * GROUP) + u * GROUP
        if u == U - 1:
            if isinstance(rnd, int):
                return start - (rnd // (self.rounds - 1)) * self.overlap
            k = (self.rounds - 1).bit_length()
            start = start - ((rnd + ((1 << k) - self.rounds + 1)) >> k) * self.overlap
            return start.with_bounds(min_val=0, max_val=self.e - GROUP)
        return start


class Chain:

    def __init__(self, engine, sem):
        self.engine, self.sem, self.n = engine, sem, 0

    def __call__(self, ins):
        self.n += 1
        ins.then_inc(self.sem, 1)
        self.engine.wait_ge(self.sem, self.n)


class StageSemaphores:

    def __init__(self, nc, ctx):
        self.nc, self.all = nc, []
        ctx.callback(self.release)

    def new(self, name):
        self.all.append(self.nc.alloc_semaphore(name))
        return self.all[-1]

    def release(self):
        self.nc.clear_and_free_semaphores(self.all)
        self.nc.all_engine_barrier()


class Core:

    def __init__(self, nc, ctx, sh):
        self.nc, self.sh = nc, sh

        def sb(name, shape, dt=F32):
            return ctx.enter_context(nc.sbuf_tensor(name, shape, dt))

        self.ident = sb("ident", [P, P])
        self.iota = sb("iota", [P, WIN])
        self.eps = sb("eps", [P, 1])
        self.one = sb("one", [P, 1])
        self.x = sb("x_nodes", [P, sh.blocks, D])
        self.h_flat = sb("h_nodes", [P, sh.cols])
        self.h = self.h_flat[:, 0:sh.rows].rearrange("p (b d) -> p b d", d=D)
        self.acc = sb("acc", [P, sh.cols])
        self.rel0 = sb("rel0", [P, sh.groups, J])
        self.base0 = sb("base0", [1, sh.groups], I32)
        self.windows = sb("windows", [1, 1], I32)
        self.deg = sb("deg", [P, sh.blocks])
        self.dinv = sb("dinv", [P, sh.blocks])
        self.dinv9 = sb("dinv9", [P, sh.blocks])


def setup_stage(nc, core, x, dst):
    sh = core.sh
    with ExitStack() as ctx:
        sems_of = StageSemaphores(nc, ctx)
        def sb(name, shape, dt=F32):
            return ctx.enter_context(nc.sbuf_tensor(name, shape, dt))

        def sem(name):
            return sems_of.new(name)

        G = sh.groups
        dst_i = sb("dst_i", [P, G, J], I32)
        low = sb("low", [P, G])
        high = sb("high", [P, G])
        iota_i = sb("iota_i", [P, WIN], I32)
        col = sb("col", [P, 4])
        base_f = sb("base_f", [1, G])
        top_f = sb("top_f", [1, G])
        ones_row = sb("ones_row", [1, P])
        span = sb("span", [1, 4])
        span_i = sb("span_i", [1, 4], I32)
        pt = ctx.enter_context(nc.psum_tensor("pt", [P, 4, 512], F32))
        dst_loaded = sem("dst_loaded")
        x_loaded = sem("x_loaded")
        tail_zero = sem("tail_zero")
        consts_pool = sem("consts_pool")
        bounds_ready = sem("bounds_ready")
        turned = sem("turned")
        cols_ready = sem("cols_ready")
        rows_turned = sem("rows_turned")
        row_ready = sem("row_ready")
        spread = sem("spread")
        chain_pool = sem("chain_pool")
        chain_dve = sem("chain_dve")
        block = ctx.enter_context(nc.Block())
        parts = [(at, min(P, G - at)) for at in range(0, G, P)]

        @block.sync
        def _(sp):
            whole = (G - 1) * GROUP
            sp.dma_start(dst_i[:, 0:G - 1, :],
                         dst[0:whole].rearrange("(g p j) -> p g j", p=P, j=J)).then_inc(dst_loaded, DMA)
            sp.dma_start(dst_i[:, G - 1, :],
                         dst[sh.e - GROUP:sh.e].rearrange("(p j) -> p j", j=J)).then_inc(dst_loaded, DMA)
            full = (sh.blocks - 1) * P
            sp.dma_start(core.x[:, 0:sh.blocks - 1, :],
                         x[0:full, :].rearrange("(b p) d -> p b d", p=P)).then_inc(x_loaded, DMA)
            sp.wait_ge(tail_zero, 1)
            sp.dma_start(core.x[0:sh.last_block, sh.blocks - 1, :], x[full:sh.n, :]).then_inc(x_loaded, DMA)
            sp.wait_ge(x_loaded, 2 * DMA)

        @block.gpsimd
        def _(pool):
            link = Chain(pool, chain_pool)
            link(nc.gpsimd.memset(core.ident[:, :], 0.0))
            nc.gpsimd.affine_select(out=core.ident[:, :], in_=core.ident[:, :], compare_op=ALU.not_equal,
                                    fill=1.0, base=0, pattern=[[-1, P]],
                                    channel_multiplier=1).then_inc(consts_pool, 1)
            nc.gpsimd.iota(iota_i[:, :], pattern=[[1, WIN]], base=0, channel_multiplier=0).then_inc(consts_pool, 1)

        @block.vector
        def _(dve):
            link = Chain(dve, chain_dve)
            nc.vector.memset(core.x[:, sh.blocks - 1, :], 0.0).then_inc(tail_zero, 1)
            nc.vector.memset(core.acc[:, :], 0.0)
            nc.vector.memset(core.eps[:, :], EPS)
            nc.vector.memset(core.one[:, :], 1.0)
            link(nc.vector.memset(ones_row[:, :], 1.0))
            dve.wait_ge(dst_loaded, 2 * DMA)
            link(nc.vector.tensor_copy(core.rel0[:, :, :], dst_i[:, :, :]))
            nc.vector.tensor_reduce(low[:, :], core.rel0[:, :, :], AX.X, ALU.min).then_inc(bounds_ready, 1)
            nc.vector.tensor_reduce(high[:, :], core.rel0[:, :, :], AX.X, ALU.max).then_inc(bounds_ready, 1)
            dve.wait_ge(consts_pool, 2)
            nc.vector.tensor_copy(core.iota[:, :], iota_i[:, :])
            dve.wait_ge(turned, 2 * len(parts))
            last = None
            for i, (at, k) in enumerate(parts):
                nc.vector.tensor_reduce(col[0:k, 2 * i:2 * i + 1], pt[0:k, 0, i * P:(i + 1) * P], AX.X, ALU.min)
                last = nc.vector.tensor_reduce(col[0:k, 2 * i + 1:2 * i + 2], pt[0:k, 1, i * P:(i + 1) * P], AX.X, ALU.max)
            last.then_inc(cols_ready, 1)
            dve.wait_ge(rows_turned, 1)
            link(nc.vector.tensor_copy(base_f[:, :], pt[0:1, 2, 0:G]))
            nc.vector.tensor_copy(core.base0[:, :], base_f[:, :]).then_inc(row_ready, 1)
            link(nc.vector.tensor_tensor(top_f[:, :], pt[0:1, 3, 0:G], base_f[:, :], ALU.subtract))
            link(nc.vector.tensor_reduce(span[0:1, 0:1], top_f[:, :], AX.X, ALU.max))
            link(nc.vector.tensor_copy(span_i[0:1, 0:1], span[0:1, 0:1]))
            link(nc.vector.tensor_scalar(span_i[0:1, 1:2], span_i[0:1, 0:1], WIN.bit_length() - 1, None,
                                         ALU.logical_shift_right))
            link(nc.vector.tensor_scalar(core.windows[0:1, 0:1], span_i[0:1, 1:2], 1.0, None, ALU.add))
            dve.wait_ge(spread, 1)
            link(nc.vector.tensor_tensor(core.rel0[:, :, :], core.rel0[:, :, :],
                                         pt[:, 0, 0:G].unsqueeze(2).broadcast_to([P, G, J]), ALU.subtract))
            if sh.overlap:
                nc.vector.memset(core.rel0[0:sh.overlap // J, G - 1, :], FAR)

        @block.tensor
        def _(pe):
            pe.wait_ge(consts_pool, 2)
            pe.wait_ge(bounds_ready, 2)
            for i, (at, k) in enumerate(parts):
                nc.tensor.transpose(pt[0:k, 0, i * P:(i + 1) * P], low[:, at:at + k], core.ident[:, :]).then_inc(turned, 1)
                nc.tensor.transpose(pt[0:k, 1, i * P:(i + 1) * P], high[:, at:at + k], core.ident[:, :]).then_inc(turned, 1)
            pe.wait_ge(cols_ready, 1)
            for i, (at, k) in enumerate(parts):
                nc.tensor.matmul(pt[0:1, 2, at:at + k], col[0:k, 2 * i:2 * i + 1], core.ident[0:k, 0:k],
                                 start=True, stop=True)
                last = nc.tensor.matmul(pt[0:1, 3, at:at + k], col[0:k, 2 * i + 1:2 * i + 2], core.ident[0:k, 0:k],
                                        start=True, stop=True)
            last.then_inc(rows_turned, 1)
            pe.wait_ge(row_ready, 1)
            nc.tensor.matmul(pt[:, 0, 0:G], ones_row[0:1, :], base_f[0:1, :], start=True, stop=True).then_inc(spread, 1)


class Windows:

    def __init__(self, nc, ctx, sems_of, core, tag):
        sh = core.sh
        self.nc, self.core = nc, core
        self.rel = ctx.enter_context(nc.sbuf_tensor(f"rel_{tag}", [P, sh.groups, J], F32))
        self.base = ctx.enter_context(nc.sbuf_tensor(f"base_{tag}", [1, sh.groups], I32))
        self.ready = sems_of.new(f"windows_ready_{tag}")

    def start(self):
        nc, core = self.nc, self.core
        nc.vector.tensor_copy(self.rel[:, :, :], core.rel0[:, :, :]).then_inc(self.ready, 1)
        nc.vector.tensor_copy(self.base[:, :], core.base0[:, :]).then_inc(self.ready, 1)

    def move_on(self):
        nc, sh = self.nc, self.core.sh
        nc.vector.tensor_scalar(self.rel[:, :, :], self.rel[:, :, :], float(-WIN), None,
                                ALU.add).then_inc(self.ready, 1)
        nc.vector.tensor_scalar(self.base[:, :], self.base[:, :], float(WIN), float(sh.rows), ALU.add,
                                ALU.min).then_inc(self.ready, 1)

    def wait(self, engine, w):
        engine.wait_ge(self.ready, w * 2 + 2)

    def count(self, engine):
        return engine.value_load(self.core.windows[0:1, 0:1], min_val=1, max_val=-(-self.core.sh.n // WIN) + 1)

    def start_of(self, engine, rnd, u):
        return engine.value_load(self.base[0:1, ds(rnd * U + u, 1)], min_val=0, max_val=self.core.sh.rows)


class Group:

    def __init__(self, sh, t, rnd, u):
        self.sh, self.t, self.rnd, self.u = sh, t, rnd, u
        self.s = u % 2
        self.n = t * (U // 2) + u // 2
        self.k = t * U + u

    def near(self, d):
        up, u = divmod(self.u + d, U)
        if isinstance(self.rnd, int):
            if not 0 <= self.rnd + up < self.sh.rounds:
                return None
        return Group(self.sh, self.t + up, self.rnd + up, u)


def edge_loop(sh, engine, w, body):
    for u in range(U):
        body(Group(sh, w * sh.rounds, 0, u))
    if sh.rounds > 2:
        with engine.Fori(1, sh.rounds - 1) as rnd:
            for u in range(U):
                body(Group(sh, w * sh.rounds + rnd, rnd, u))
    for u in range(U):
        body(Group(sh, w * sh.rounds + (sh.rounds - 1), sh.rounds - 1, u))


def one_hots(nc, core, win, g, out):
    rel = win.rel[:, ds(g.rnd * U + g.u, 1), :].rearrange("p a j -> p (a j)")
    return nc.vector.tensor_tensor(out, core.iota[:, :].unsqueeze(1).broadcast_to([P, J, WIN]),
                                   rel.unsqueeze(2).broadcast_to([P, J, WIN]), ALU.is_equal)


def degree_stage(nc, core):
    sh = core.sh
    with ExitStack() as ctx:
        sems_of = StageSemaphores(nc, ctx)
        def sb(name, shape, dt=F32):
            return ctx.enter_context(nc.sbuf_tensor(name, shape, dt))

        def sem(name):
            return sems_of.new(f"{name}_deg")

        win = Windows(nc, ctx, sems_of, core, "deg")
        ones_b = sb("ones_b", [P, 1], BF16)
        hot = sb("hot", [P, 2, J, WIN], BF16)
        deg_row = sb("deg_row", [1, sh.cols])
        root = sb("root", [P, sh.blocks])
        ps = [ctx.enter_context(nc.psum_tensor(f"ps{i}", [P, 512], F32)) for i in range(2)]
        pd = ctx.enter_context(nc.psum_tensor("pd", [P, 512], F32))
        consts = sem("consts")
        hot_ready = [sem(f"hot_ready{i}") for i in range(2)]
        summed = [sem(f"summed{i}") for i in range(2)]
        added = sem("added")
        turned = sem("turned")
        deg_ready = sem("deg_ready")
        root_ready = sem("root_ready")
        chain = sem("chain")
        block = ctx.enter_context(nc.Block())

        @block.vector
        def _(dve):
            nc.vector.memset(ones_b[:, :], 1.0).then_inc(consts, 1)
            nc.vector.memset(deg_row[:, :], 0.0).then_inc(consts, 1)
            win.start()
            dve.wait_ge(consts, 2)
            windows = win.count(dve)

            def add(g):
                if g is None:
                    return
                base = win.start_of(dve, g.rnd, g.u)
                dve.wait_ge(summed[g.s], g.n + 1)
                dve.wait_ge(added, g.k)
                nc.vector.tensor_tensor(deg_row[0:1, ds(base, WIN)], deg_row[0:1, ds(base, WIN)],
                                        ps[g.s][0:1, 0:WIN], ALU.add).then_inc(added, 1)

            with dve.Fori(0, windows) as w:
                def body(g):
                    win.wait(dve, w)
                    dve.wait_ge(summed[g.s], g.n)
                    one_hots(nc, core, win, g, hot[:, g.s, :, :]).then_inc(hot_ready[g.s], 1)
                    add(g.near(-1))
                    if g.near(1) is None:
                        add(g)

                edge_loop(sh, dve, w, body)
                dve.wait_ge(added, (w + 1) * sh.groups)
                win.move_on()
            dve.wait_ge(turned, 1)
            link = Chain(dve, chain)
            nc.vector.tensor_copy(core.deg[:, :], pd[:, 0:sh.blocks]).then_inc(deg_ready, 1)
            dve.wait_ge(root_ready, 1)
            link(nc.vector.reciprocal(core.dinv[:, :], root[:, :]))
            nc.vector.tensor_scalar(core.dinv9[:, :], core.dinv[:, :], 0.9, None, ALU.mult)

        @block.tensor
        def _(pe):
            pe.wait_ge(consts, 2)
            windows = win.count(pe)
            with pe.Fori(0, windows) as w:
                def body(g):
                    s = g.s
                    pe.wait_ge(hot_ready[s], g.n + 1)
                    old = g.near(-2)
                    if old:
                        pe.wait_ge(added, old.k + 1)
                    for j in range(J):
                        last = nc.tensor.matmul(ps[s][0:1, 0:WIN], ones_b[:, :], hot[:, s, j, :],
                                                start=(j == 0), stop=(j == J - 1))
                    last.then_inc(summed[s], 1)

                edge_loop(sh, pe, w, body)
            pe.wait_ge(added, windows * sh.groups)
            for b in range(sh.blocks):
                last = nc.tensor.matmul(pd[:, b:b + 1], deg_row[0:1, b * P:(b + 1) * P], core.one[0:1, :],
                                        start=True, stop=True)
            last.then_inc(turned, 1)

        @block.scalar
        def _(act):
            act.wait_ge(deg_ready, 1)
            nc.scalar.activation(root[:, :], core.deg[:, :], ACT.Sqrt, bias=core.one[:, :]).then_inc(root_ready, 1)


def gather_loop(nc, pool, win, sh, table, idx, rows, idx_loaded, rows_used, rows_loaded, group_begun):
    windows = win.count(pool)
    with pool.Fori(0, windows) as w:
        with pool.Fori(0, sh.rounds) as rnd:
            t = w * sh.rounds + rnd
            for u in range(U):
                pool.wait_ge(idx_loaded[u], t * DMA + DMA)
                pool.wait_ge(rows_used[u], t)
                pool.sem_inc(group_begun, 1)
                for j in range(J):
                    pool.indirect_dma_start(
                        out=rows[:, u, j, :], out_offset=None, in_=table,
                        in_offset=bass.IndirectOffsetOnAxis(ap=idx[:, u, j:j + 1], axis=0),
                    ).then_inc(rows_loaded[u], DMA)


def sum_pass(nc, core, src, table, tag):
    sh = core.sh
    with ExitStack() as ctx:
        sems_of = StageSemaphores(nc, ctx)
        def sb(name, shape, dt=F32):
            return ctx.enter_context(nc.sbuf_tensor(f"{name}_{tag}", shape, dt))

        def sem(name):
            return sems_of.new(f"{name}_{tag}")

        win = Windows(nc, ctx, sems_of, core, tag)
        idx = sb("idx", [P, U, J], I32)
        rows = sb("rows", [P, U, J, D])
        hot = sb("hot", [P, 2, J, WIN])
        ps = [ctx.enter_context(nc.psum_tensor(f"ps{i}_{tag}", [P, 512], F32)) for i in range(2)]
        idx_loaded = [sem(f"idx_loaded{u}") for u in range(U)]
        rows_loaded = [sem(f"rows_loaded{u}") for u in range(U)]
        rows_used = [sem(f"rows_used{u}") for u in range(U)]
        group_begun = sem("group_begun")
        hot_ready = [sem(f"hot_ready{i}") for i in range(2)]
        added = sem("added")
        block = ctx.enter_context(nc.Block())

        @block.sync
        def _(sp):
            windows = win.count(sp)
            with sp.Fori(0, windows) as w:
                with sp.Fori(0, sh.rounds) as rnd:
                    t = w * sh.rounds + rnd
                    for u in range(U):
                        sp.wait_ge(rows_loaded[u], t * (J * DMA))
                        sp.dma_start(idx[:, u, :], src[ds(sp.snap(sh.first_edge(rnd, u)), GROUP)]
                                     .rearrange("(p j) -> p j", j=J)).then_inc(idx_loaded[u], DMA)

        @block.gpsimd
        def _(pool):
            gather_loop(nc, pool, win, sh, table, idx, rows, idx_loaded, rows_used, rows_loaded, group_begun)

        @block.vector
        def _(dve):
            win.start()
            windows = win.count(dve)
            with dve.Fori(0, windows) as w:
                with dve.Fori(0, sh.rounds) as rnd:
                    t = w * sh.rounds + rnd
                    win.wait(dve, w)
                    for u in range(U):
                        s = u % 2
                        if u >= 2:
                            dve.wait_ge(rows_used[u - 2], t + 1)
                        else:
                            dve.wait_ge(rows_used[u + 2], t)
                        one_hots(nc, core, win, Group(sh, t, rnd, u), hot[:, s, :, :]).then_inc(hot_ready[s], 1)
                        base = win.start_of(dve, rnd, u)
                        dve.wait_ge(rows_used[u], t + 1)
                        dve.wait_ge(added, t * U + u)
                        nc.vector.tensor_tensor(core.acc[:, ds(base, WIN)], core.acc[:, ds(base, WIN)],
                                                ps[s][:, 0:WIN], ALU.add).then_inc(added, 1)
                dve.wait_ge(added, (w + 1) * sh.groups)
                win.move_on()

        @block.tensor
        def _(pe):
            windows = win.count(pe)
            with pe.Fori(0, windows) as w:
                with pe.Fori(0, sh.rounds) as rnd:
                    t = w * sh.rounds + rnd
                    for u in range(U):
                        s = u % 2
                        pe.wait_ge(hot_ready[s], t * (U // 2) + u // 2 + 1)
                        pe.wait_ge(rows_loaded[u], (t + 1) * (J * DMA))
                        pe.wait_ge(added, t * U + u - 1 if u >= 2 else t * U)
                        for j in range(J):
                            last = nc.tensor.matmul(ps[s][:, 0:WIN], rows[:, u, j, :], hot[:, s, j, :],
                                                    start=(j == 0), stop=(j == J - 1))
                        last.then_inc(rows_used[u], 1)


class LoopChain:

    def __init__(self, engine, sem, rnd, steps):
        self.engine, self.sem, self.rnd, self.steps, self.n = engine, sem, rnd, steps, 0

    def __call__(self, ins):
        self.n += 1
        ins.then_inc(self.sem, 1)
        self.engine.wait_ge(self.sem, self.rnd * self.steps + self.n)

    def end(self):
        assert self.n == self.steps, self.n


def spread(col, k=D):
    return col.unsqueeze(2).broadcast_to([P, NB, k])


def moments(nc, link, src, stats, mv, begun):
    for b in range(NB):
        last = nc.vector.bn_stats(stats[:, b, :], src[:, b, :])
    link(last)
    link.engine.sem_inc(begun, 1)
    for b in range(NB):
        last = nc.vector.bn_aggr(mv[:, b, :], stats[:, b, :])
    return last


def node_stage(nc, core, layer, table=None, table_t=None, out=None, att=None, w=None):
    sh = core.sh
    tag = f"n{layer}"
    with ExitStack() as ctx:
        sems_of = StageSemaphores(nc, ctx)
        def sb(name, shape, dt=F32):
            return ctx.enter_context(nc.sbuf_tensor(f"{name}_{tag}", shape, dt))

        def sem(name):
            return sems_of.new(f"{name}_{tag}")

        def psum(name, free):
            return ctx.enter_context(nc.psum_tensor(f"{name}_{tag}", [P] + free, F32))

        width = 132 if layer == 2 else D
        a = sb("a", [P, NB, D])
        stats = sb("stats", [P, NB, 6])
        mv = sb("mv", [P, NB, 2])
        std = sb("std", [P, NB])
        rstd = sb("rstd", [P, NB])
        shift = sb("shift", [P, NB])
        tab = sb("tab", [P, NB, width])
        tab_t = sb("tab_t", [P, NB, 4]) if layer == 2 else None
        hT = sb("hT", [P, NB, P]) if layer in (2, 4) else None
        pt = psum("pt", [NB + 1, D])
        ph = psum("ph", [NB + 1, P]) if layer in (2, 4) else None
        pw = psum("pw", [NB + 1, D]) if layer == 4 else None
        pw2 = psum("pw2", [3, 512]) if layer == 2 else None
        turned = sem("turned")
        taken = sem("taken")
        var_ready = sem("var_ready")
        std_ready = sem("std_ready")
        scale_ready = sem("scale_ready")
        h_ready = sem("h_ready")
        tab_ready = sem("tab_ready")
        stored = sem("stored")
        chain = sem("chain")
        begun = sem("begun")
        h_turned = sem("h_turned")
        hT_ready = sem("hT_ready")
        product = sem("product")
        em_ready = sem("em_ready")
        m_taken = sem("m_taken")
        if layer == 3:
            sc = sb("sc", [P, NB, 8])
            em = sb("em", [P, NB, 4])
            rest = sb("rest", [P, NB])
            pd = psum("pd", [NB + 1, 8])
        if layer == 4:
            rdeg = sb("rdeg", [P, sh.blocks])
            some = sb("some", [P, sh.blocks])
            b = sb("b", [P, NB, D])
        block = ctx.enter_context(nc.Block())
        rounds = sh.node_rounds

        if layer > 0:
            @block.tensor
            def _(pe):
                for r in range(rounds):
                    if r:
                        pe.wait_ge(taken, r)
                    for b_ in range(NB):
                        acc_b = core.acc[:, (r * NB + b_) * P:(r * NB + b_ + 1) * P]
                        if layer == 4:
                            last = nc.tensor.matmul(pt[:, b_, :], acc_b, w.msg[:, :], start=True, stop=True)
                        else:
                            last = nc.tensor.transpose(pt[:, b_, :], acc_b, core.ident[:, :])
                    if layer == 3:
                        for b_ in range(NB):
                            at = slice((r * NB + b_) * P, (r * NB + b_ + 1) * P)
                            nc.tensor.transpose(pd[:, b_, 0:4], att.den[:, at], core.ident[0:4, 0:4])
                            last = nc.tensor.transpose(pd[:, b_, 4:8], att.top[:, at], core.ident[0:4, 0:4])
                    last.then_inc(turned, 1)
                    if layer in (2, 4):
                        if layer == 2:
                            pe.wait_ge(h_ready, r + 1)
                        for b_ in range(NB):
                            last = nc.tensor.transpose(ph[:, b_, :], core.h[:, r * NB + b_, :], core.ident[:, :])
                        last.then_inc(h_turned, 1)
                        pe.wait_ge(hT_ready, r + 1)
                        for b_ in range(NB):
                            if layer == 2:
                                last = nc.tensor.matmul(pw2[:, b_ // 3, (b_ % 3) * 136:(b_ % 3) * 136 + 136],
                                                        hT[:, b_, :], w.att[:, :], start=True, stop=True)
                            else:
                                last = nc.tensor.matmul(pw[:, b_, :], hT[:, b_, :], w.self_[:, :], start=True, stop=True)
                        last.then_inc(product, 1)

        @block.scalar
        def _(act):
            with act.Fori(0, rounds) as r:
                if layer == 3:
                    act.wait_ge(m_taken, r + 1)
                    nc.scalar.activation(em[:, :, :], sc[:, :, 4:8], ACT.Exp, scale=-1.0).then_inc(em_ready, 1)
                if layer == 4:
                    act.wait_ge(h_turned, r + 1)
                    nc.scalar.copy(hT[:, :, :], ph[:, 0:NB, :]).then_inc(hT_ready, 1)
                act.wait_ge(var_ready, r + 1)
                nc.scalar.activation(std[:, :], mv[:, :, 1], ACT.Sqrt, bias=core.eps[:, :]).then_inc(std_ready, 1)
                act.wait_ge(scale_ready, r + 1)
                if layer == 1:
                    act.wait_ge(stored, r * DMA)
                for b_ in range(NB):
                    rs, sf = rstd[:, b_:b_ + 1], shift[:, b_:b_ + 1]
                    if layer == 4:
                        last = nc.scalar.activation(a[:, b_, :], b[:, b_, :], ACT.Identity, scale=rs, bias=sf)
                        continue
                    xin = core.x[:, ds(r * NB + b_, 1), :].rearrange("p a d -> p (a d)")
                    if layer == 1:
                        nc.scalar.activation(tab[:, b_, 0:32], xin[:, 0:32], ACT.Relu, scale=rs, bias=sf)
                        last = nc.scalar.activation(tab[:, b_, 32:128].rearrange("p (i u) -> p u i", i=3),
                                                    xin[:, 32:128].rearrange("p (u i) -> p u i", i=3),
                                                    ACT.Relu, scale=rs, bias=sf)
                    else:
                        hout = core.h[:, ds(r * NB + b_, 1), :].rearrange("p a d -> p (a d)")
                        last = nc.scalar.activation(hout, xin, ACT.Relu, scale=rs, bias=sf)
                last.then_inc(h_ready, 1)
                if layer == 2:
                    act.wait_ge(h_turned, r + 1)
                    nc.scalar.copy(hT[:, :, :], ph[:, 0:NB, :]).then_inc(hT_ready, 1)

        @block.vector
        def _(dve):
            if layer == 4:
                link0 = Chain(dve, tab_ready)
                link0(nc.vector.tensor_scalar(rdeg[:, :], core.deg[:, :], 1.0, None, ALU.max))
                link0(nc.vector.reciprocal(rdeg[:, :], rdeg[:, :]))
                link0(nc.vector.tensor_tensor(some[:, :], rdeg[:, :], core.deg[:, :], ALU.mult))
            with dve.Fori(0, rounds) as r:
                nodes = ds(r * NB, NB)
                x, h = core.x[:, nodes, :], core.h[:, nodes, :]
                steps = {0: 3, 1: 8, 2: 4, 3: 8, 4: 9}[layer]
                link = LoopChain(dve, chain, r, steps)
                src = x
                if layer > 0:
                    dve.wait_ge(turned, r + 1)
                if layer == 1:
                    link(nc.vector.tensor_tensor(a[:, :, :], h, spread(core.dinv[:, nodes]), ALU.mult))
                    link(nc.vector.tensor_tensor(a[:, :, :], a[:, :, :], pt[:, 0:NB, :], ALU.add))
                    link(nc.vector.tensor_tensor(a[:, :, :], a[:, :, :], spread(core.dinv9[:, nodes]), ALU.mult))
                    link(nc.vector.scalar_tensor_tensor(a[:, :, :], h, 0.1, a[:, :, :], ALU.mult, ALU.add))
                    link(nc.vector.scalar_tensor_tensor(a[:, :, :], a[:, :, :], 0.0, h, ALU.max, ALU.add))
                    link(nc.vector.tensor_tensor(x, x, a[:, :, :], ALU.add))
                if layer == 2:
                    link(nc.vector.tensor_tensor(x, x, pt[:, 0:NB, :], ALU.add))
                if layer == 3:
                    nc.vector.tensor_copy(sc[:, :, :], pd[:, 0:NB, :]).then_inc(m_taken, 1)
                    link(nc.vector.tensor_scalar(rest[:, :], core.deg[:, nodes], -1.0, float(sh.e), ALU.mult, ALU.add))
                    dve.wait_ge(m_taken, r + 1)
                    dve.wait_ge(em_ready, r + 1)
                    link(nc.vector.tensor_tensor(em[:, :, :], em[:, :, :], spread(rest[:, :], 4), ALU.mult))
                    link(nc.vector.tensor_tensor(em[:, :, :], em[:, :, :], sc[:, :, 0:4], ALU.add))
                    link(nc.vector.reciprocal(em[:, :, :], em[:, :, :]))
                    heads = [P, NB * 4, 32]
                    link(nc.vector.tensor_tensor(a[:, :, :].rearrange("p b (h c) -> p (b h) c", h=4),
                                                 pt[:, 0:NB, :].rearrange("p b (h c) -> p (b h) c", h=4),
                                                 em[:, :, :].rearrange("p b h -> p (b h)").unsqueeze(2).broadcast_to(heads),
                                                 ALU.mult))
                    link(nc.vector.tensor_tensor(x, x, a[:, :, :], ALU.add))
                if layer == 4:
                    link(nc.vector.tensor_tensor(b[:, :, :], pt[:, 0:NB, :], spread(rdeg[:, nodes]), ALU.mult))
                    dve.wait_ge(product, r + 1)
                    link(nc.vector.tensor_tensor(b[:, :, :], b[:, :, :], pw[:, 0:NB, :], ALU.add))
                    def row(i):
                        return w.rows[:, i:i + 1, :].broadcast_to([P, NB, D])

                    dve.wait_ge(h_ready, r)
                    link(nc.vector.tensor_tensor(a[:, :, :], row(1), spread(some[:, nodes]), ALU.mult))
                    link(nc.vector.tensor_tensor(b[:, :, :], b[:, :, :], a[:, :, :], ALU.add))
                    link(nc.vector.tensor_tensor(b[:, :, :], b[:, :, :], row(0), ALU.add))
                    src = b
                dve.sem_inc(begun, 1)
                moments(nc, link, src, stats, mv, begun).then_inc(var_ready, 1)
                dve.wait_ge(var_ready, r + 1)
                dve.wait_ge(std_ready, r + 1)
                link(nc.vector.reciprocal(rstd[:, :], std[:, :]))
                if layer > 0:
                    nc.vector.scalar_tensor_tensor(shift[:, :], mv[:, :, 0], -1.0, rstd[:, :], ALU.mult, ALU.mult).then_inc(scale_ready, 1)
                else:
                    nc.vector.scalar_tensor_tensor(shift[:, :], mv[:, :, 0], -1.0, rstd[:, :], ALU.mult, ALU.mult).then_inc(scale_ready, 1)
                dve.wait_ge(h_ready, r + 1)
                if layer == 0:
                    dve.wait_ge(stored, r * DMA)
                    link(nc.vector.tensor_tensor(tab[:, :, :], h, spread(core.dinv[:, nodes]), ALU.mult))
                if layer == 2:
                    dve.wait_ge(product, r + 1)
                    dve.wait_ge(stored, r * (2 * DMA))
                    for b_ in range(NB):
                        p0 = (b_ % 3) * 136
                        nc.vector.tensor_copy(tab[:, b_, :], pw2[:, b_ // 3, p0:p0 + 132])
                        last = nc.vector.tensor_copy(tab_t[:, b_, :], pw2[:, b_ // 3, p0 + 132:p0 + 136])
                    link(last)
                if layer == 4:
                    link(nc.vector.tensor_tensor(a[:, :, :], a[:, :, :], row(2), ALU.mult))
                    link(nc.vector.tensor_tensor(a[:, :, :], a[:, :, :], row(3), ALU.add))
                    nc.vector.scalar_tensor_tensor(x, a[:, :, :], 0.0, x, ALU.max, ALU.add).then_inc(taken, 1)
                    dve.wait_ge(taken, r + 1)
                elif layer > 0:
                    dve.sem_inc(taken, 1)
                link.end()
            if 0 < layer < 4:
                nc.vector.memset(core.acc[:, :], 0.0)

        @block.sync
        def _(sp):
            span = NB * P
            if layer == 4:
                if rounds > 1:
                    with sp.Fori(0, rounds - 1) as r:
                        sp.wait_ge(taken, r + 1)
                        sp.dma_start(out[ds(r * span, span), :].rearrange("(b p) d -> p b d", p=P),
                                     core.x[:, ds(r * NB, NB), :]).then_inc(stored, DMA)
                whole = (sh.blocks - 1) * P
                sp.wait_ge(taken, rounds)
                sp.dma_start(out[(rounds - 1) * span:whole, :].rearrange("(b p) d -> p b d", p=P),
                             core.x[:, (rounds - 1) * NB:sh.blocks - 1, :]).then_inc(stored, DMA)
                sp.dma_start(out[whole:sh.n, :], core.x[0:sh.last_block, sh.blocks - 1, :]).then_inc(stored, DMA)
                sp.wait_ge(stored, (rounds + 1) * DMA)
                return
            with sp.Fori(0, rounds) as r:
                if layer in (0, 2):
                    sp.wait_ge(chain, (r + 1) * (3 if layer == 0 else 4))
                else:
                    sp.wait_ge(h_ready, r + 1)
                rows = table[ds(r * span, span), :].rearrange("(b p) d -> p b d", p=P)
                what = core.h[:, ds(r * NB, NB), :] if layer == 3 else tab[:, :, :]
                sp.dma_start(rows, what).then_inc(stored, DMA)
                if layer == 2:
                    rows_t = table_t[ds(r * span, span), :].rearrange("(b p) d -> p b d", p=P)
                    sp.dma_start(rows_t, tab_t[:, :, :]).then_inc(stored, DMA)
            sp.wait_ge(stored, rounds * DMA * (2 if layer == 2 else 1))
            if layer == 2:
                sp.dma_start(table_t[sh.rows:sh.cols, :], core.ident[:, 0:4]).then_inc(stored, DMA)
                sp.wait_ge(stored, (2 * rounds + 1) * DMA)


NEIGHBOURS = 10.0
MUL = 32
NORM_S = (1.0 / (2 * MUL)) ** 0.5 / NEIGHBOURS ** 0.5
NORM_V = (3.0 / (3 * MUL)) ** 0.5 / NEIGHBOURS ** 0.5
PATHS = [NORM_S, NORM_V / 3 ** 0.5, NORM_V / 3 ** 0.5, NORM_S / 3 ** 0.5, NORM_V / 10 ** 0.5]


class Weights:
    def __init__(self, nc, ctx):
        def sb(name, shape, dt=F32):
            return ctx.enter_context(nc.sbuf_tensor(name, shape, dt))

        self.mix = sb("w_mix", [P, 3, D])
        self.att = sb("w_att", [P, 136])
        self.edge = sb("w_edge", [P, 8])
        self.msg = sb("w_msg", [P, D])
        self.self_ = sb("w_self", [P, D])
        self.ident_b = sb("w_ident_b", [P, P], BF16)
        self.pick = sb("w_pick", [96, 32, P], BF16)
        self.heads = sb("w_heads", [4, D])
        self.rows = sb("w_rows", [P, 4, D])


def weights_stage(nc, core, w, a):
    with ExitStack() as ctx:
        sems_of = StageSemaphores(nc, ctx)
        def sb(name, shape, dt=F32):
            return ctx.enter_context(nc.sbuf_tensor(name, shape, dt))

        def sem(name):
            return sems_of.new(name)

        raw = sb("raw", [P, 3, MUL])
        node = sb("node", [P, P])
        edge = sb("edge", [P, 2, 64])
        att_a = sb("att_a", [P, 12])
        pn = ctx.enter_context(nc.psum_tensor("pn", [P, 512], F32))
        zeroed = sem("zeroed")
        loaded = sem("loaded")
        products = sem("products")
        block = ctx.enter_context(nc.Block())
        loads = []

        @block.sync
        def _(sp):
            for at, k in ((0, 0), (32, 2), (64, 2), (96, 2)):
                loads.append((raw[at:at + 32, 0, :], a[f"L1_gnn_w{k}"]))
            for at, k in ((0, 1), (32, 1), (64, 1), (96, 3)):
                loads.append((raw[at:at + 32, 1, :], a[f"L1_gnn_w{k}"]))
            for at, k in ((0, 4), (32, 4), (64, 4), (96, 3)):
                loads.append((raw[at:at + 32, 2, :], a[f"L1_gnn_w{k}"]))
            loads2 = [(dst, src.rearrange("u a w -> u (a w)")) for dst, src in loads]
            loads2.append((node[:, :], a["L2_gnn_W_node"]))
            loads2.append((edge[:, 0, :], a["L2_gnn_W_edge"]))
            loads2.append((edge[:, 1, :], a["L2_gnn_W_edge"]))
            loads2.append((w.msg[:, :], a["L3_gnn_W_msg"]))
            loads2.append((w.self_[:, :], a["L3_gnn_W_self"]))
            for i, name in enumerate(("b_self", "b_msg", "ln_gamma", "ln_beta")):
                loads2.append((w.rows[:, i, :], a[f"L3_gnn_{name}"].unsqueeze(0).broadcast_to([P, D])))
            for dst, src in loads2:
                sp.dma_start(dst, src).then_inc(loaded, DMA)
            sp.wait_ge(zeroed, 2)
            n = len(loads2)
            with nc.allow_non_contiguous_dma(reason="twelve columns of 32 values"):
                for h in range(4):
                    for i in range(3):
                        sp.dma_start(att_a[32 * h:32 * h + 32, 4 * i + h:4 * i + h + 1],
                                     a["L2_gnn_a"][h:h + 1, 32 * i:32 * i + 32].rearrange("a c -> c a")).then_inc(loaded, DMA)
                        n += 1
            sp.wait_ge(loaded, n * DMA)
            sp.sem_inc(zeroed, 1)

        @block.vector
        def _(dve):
            nc.vector.memset(w.edge[:, :], 0.0)
            nc.vector.memset(w.mix[:, :, :], 0.0).then_inc(zeroed, 1)
            nc.vector.memset(att_a[:, :], 0.0).then_inc(zeroed, 1)
            dve.wait_ge(zeroed, 3)
            vec = w.mix[:, :, 32:128].rearrange("p k (w i) -> p k w i", i=3)
            nc.vector.tensor_scalar(w.mix[0:32, 0, 0:32], raw[0:32, 0, :], PATHS[0], None, ALU.mult)
            for i in range(3):
                lo = 32 + 32 * i
                nc.vector.tensor_scalar(vec[lo:lo + 32, 0, :, i], raw[lo:lo + 32, 0, :], PATHS[2], None, ALU.mult)
                lo = 32 * i
                nc.vector.tensor_scalar(vec[lo:lo + 32, 1, :, i], raw[lo:lo + 32, 1, :], PATHS[1], None, ALU.mult)
                nc.vector.tensor_scalar(vec[lo:lo + 32, 2, :, i], raw[lo:lo + 32, 2, :], PATHS[4], None, ALU.mult)
            for k in (1, 2):
                nc.vector.tensor_scalar(w.mix[96:128, k, 0:32], raw[96:128, k, :], PATHS[3], None, ALU.mult)
            dve.wait_ge(products, 1)
            nc.vector.tensor_copy(w.att[:, :], pn[:, 0:136])
            nc.vector.tensor_copy(w.edge[0:64, 0:4], pn[0:64, 136:140])
            nc.vector.tensor_copy(w.edge[64:128, 4:8], pn[64:128, 136:140])

        @block.scalar
        def _(act):
            nc.scalar.copy(w.ident_b[:, :], core.ident[:, :])
            for i in range(3):
                at = slice(32 * i, 32 * i + 32)
                nc.scalar.copy(w.pick[at, :, :], core.ident[at, at].unsqueeze(2).broadcast_to([32, 32, P]))
            nc.scalar.copy(w.heads[:, :].rearrange("h (g c) -> h g c", g=4),
                           core.ident[0:4, 0:4].unsqueeze(2).broadcast_to([4, 4, 32]))

        @block.tensor
        def _(pe):
            pe.wait_ge(zeroed, 3)
            nc.tensor.transpose(pn[:, 0:128], node[:, :], core.ident[:, :])
            nc.tensor.matmul(pn[:, 128:136], node[:, :], att_a[:, 0:8], start=True, stop=True)
            nc.tensor.matmul(pn[:, 136:140], edge[:, :, :].rearrange("p a k -> p (a k)"), att_a[:, 8:12],
                             start=True, stop=True).then_inc(products, 1)


def tensor_pass(nc, core, w_mix, src, attr, table):
    sh = core.sh
    K = 9
    with ExitStack() as ctx:
        sems_of = StageSemaphores(nc, ctx)
        def sb(name, shape, dt=F32):
            return ctx.enter_context(nc.sbuf_tensor(f"{name}_l1", shape, dt))

        def sem(name):
            return sems_of.new(f"{name}_l1")

        def sems(name, n):
            return [sem(f"{name}{i}") for i in range(n)]

        win = Windows(nc, ctx, sems_of, core, "l1")
        idx = sb("idx", [P, U, J], I32)
        rows = sb("rows", [P, U, J, D])
        ea = sb("ea", [P, U, J, 9])
        hot = sb("hot", [P, 2, J, WIN])
        m9 = sb("m9", [P, 2, J, 9])
        mid = sb("mid", [P, 2, J, 3, D])
        part = sb("part", [P, 2, J, 3, 32])
        dots = sb("dots", [P, J, 2, 32])
        agg = sb("agg", [P, 2, 3, WIN])
        ps = [ctx.enter_context(nc.psum_tensor(f"ps{i}_l1", [P, 4, WIN], F32)) for i in range(2)]
        pw = [ctx.enter_context(nc.psum_tensor(f"pw{i}_l1", [P, 512], F32)) for i in range(2)]
        idx_loaded = sems("idx_loaded", U)
        ea_loaded = sems("ea_loaded", U)
        rows_loaded = sems("rows_loaded", U)
        group_begun = sem("group_begun")
        m9_ready = sems("m9_ready", 2)
        rows_used_dve = sems("rows_used_dve", U)
        products_done = sems("products_done", 2)
        scaled = sems("scaled", U)
        summed = sems("summed", 2)
        agg_ready = sems("agg_ready", 2)
        mixed = sems("mixed", 2)
        added = sem("added")
        chain = sem("chain")
        block = ctx.enter_context(nc.Block())

        @block.sync
        def _(sp):
            windows = win.count(sp)
            with sp.Fori(0, windows) as w:
                with sp.Fori(0, sh.rounds) as rnd:
                    t = w * sh.rounds + rnd
                    for u in range(U):
                        at = ds(sp.snap(sh.first_edge(rnd, u)), GROUP)
                        sp.wait_ge(rows_loaded[u], t * (J * DMA))
                        sp.dma_start(idx[:, u, :], src[at].rearrange("(p j) -> p j", j=J)).then_inc(idx_loaded[u], DMA)
                        sp.wait_ge(scaled[u], t)
                        sp.wait_ge(rows_used_dve[u], t)
                        sp.dma_start(ea[:, u, :, :], attr[at, :].rearrange("(p j) k -> p j k", j=J)).then_inc(ea_loaded[u], DMA)

        @block.gpsimd
        def _(pool):
            windows = win.count(pool)
            with pool.Fori(0, windows) as w:
                with pool.Fori(0, sh.rounds) as rnd:
                    t = w * sh.rounds + rnd
                    for u in range(U):
                        pool.wait_ge(idx_loaded[u], t * DMA + DMA)
                        pool.wait_ge(scaled[u], t)
                        pool.wait_ge(rows_used_dve[u], t)
                        pool.sem_inc(group_begun, 1)
                        for j in range(J):
                            pool.indirect_dma_start(
                                out=rows[:, u, j, :], out_offset=None, in_=table,
                                in_offset=bass.IndirectOffsetOnAxis(ap=idx[:, u, j:j + 1], axis=0),
                            ).then_inc(rows_loaded[u], DMA)

        @block.scalar
        def _(act):
            windows = win.count(act)

            def body(g):
                u, s = g.u, g.s
                act.wait_ge(ea_loaded[u], g.t * DMA + DMA)
                act.wait_ge(products_done[s], g.n)
                t5 = ea[:, u, :, 4:9]
                for at, step, k in ((1, 2, 1), (2, 4, 0), (5, 2, 3)):
                    nc.scalar.copy(m9[:, s, :, at:at + step + 1:step], t5[:, :, k:k + 1].broadcast_to([P, J, 2]))
                nc.scalar.mul(m9[:, s, :, 4], t5[:, :, 2], 2.0 / 3 ** 0.5).then_inc(m9_ready[s], 1)
                act.wait_ge(rows_loaded[u], (g.t + 1) * (J * DMA))
                act.wait_ge(summed[s], g.n)
                for j in range(J):
                    nc.scalar.activation(mid[:, s, j, 0, :], rows[:, u, j, :], ACT.Copy, scale=ea[:, u, j, 0:1])
                    last = nc.scalar.activation(mid[:, s, j, 1, 96:128], rows[:, u, j, 32:64], ACT.Copy, scale=ea[:, u, j, 1:2])
                last.then_inc(scaled[u], 1)

            def move_sums(g):
                if g is None:
                    return
                act.wait_ge(summed[g.s], g.n + 1)
                act.wait_ge(mixed[g.s], g.n)
                nc.scalar.copy(agg[:, g.s, :, :], ps[g.s][:, 0:3, :]).then_inc(agg_ready[g.s], 1)

            def both(g):
                body(g)
                move_sums(g.near(-1))
                if g.near(1) is None:
                    move_sums(g)

            with act.Fori(0, windows) as w:
                edge_loop(sh, act, w, both)

        @block.vector
        def _(dve):
            win.start()
            windows = win.count(dve)

            def products(g, w):
                u, s = g.u, g.s
                n = [0]

                def step(ins):
                    n[0] += 1
                    ins.then_inc(chain, 1)
                    return n[0]

                def wait(k):
                    dve.wait_ge(chain, g.k * K + k)

                win.wait(dve, w)
                dve.wait_ge(summed[s], g.n)
                step(one_hots(nc, core, win, g, hot[:, s, :, :]))
                dve.wait_ge(ea_loaded[u], g.t * DMA + DMA)
                dve.wait_ge(m9_ready[s], g.n + 1)
                t5 = ea[:, u, :, 4:9]
                step(nc.vector.scalar_tensor_tensor(m9[:, s, :, 0], t5[:, :, 2], -(3 ** -0.5), t5[:, :, 4], ALU.mult, ALU.subtract))
                d = step(nc.vector.scalar_tensor_tensor(m9[:, s, :, 8], t5[:, :, 2], -(3 ** -0.5), t5[:, :, 4], ALU.mult, ALU.add))
                dve.wait_ge(rows_loaded[u], (g.t + 1) * (J * DMA))
                row = rows[:, u, :, :]
                v = ea[:, u, :, 1:4]

                def comp(i, k=3):
                    return row[:, :, 32 + 32 * i:64 + 32 * i].unsqueeze(2).broadcast_to([P, J, k, 32])

                wide = [P, J, 3, 32]
                c4 = mid[:, s, :, 2, 0:96].rearrange("p j (k u) -> p j k u", k=3)
                wait(d)

                def m_row(i):
                    return m9[:, s, :, 3 * i:3 * i + 3].unsqueeze(3).broadcast_to(wide)

                p0 = step(nc.vector.tensor_tensor(c4, comp(0), m_row(0), ALU.mult))
                p1 = step(nc.vector.tensor_tensor(part[:, 0, :, :, :], comp(1), m_row(1), ALU.mult))
                p2 = step(nc.vector.tensor_tensor(part[:, 1, :, :, :], comp(2), m_row(2), ALU.mult))
                dt = step(nc.vector.tensor_tensor(dots[:, :, :, :],
                                                  row[:, :, 64:128].rearrange("p j (i u) -> p j i u", i=2),
                                                  v[:, :, 1:3].unsqueeze(3).broadcast_to([P, J, 2, 32]), ALU.mult))
                wait(p1)
                q = step(nc.vector.tensor_tensor(c4, c4, part[:, 0, :, :, :], ALU.add))
                nc.vector.tensor_tensor(mid[:, s, :, 1, 0:96].rearrange("p j (k u) -> p j k u", k=3),
                                        row[:, :, 0:32].unsqueeze(2).broadcast_to(wide),
                                        v.unsqueeze(3).broadcast_to(wide), ALU.mult).then_inc(rows_used_dve[u], 1)
                wait(dt)
                r = step(nc.vector.tensor_tensor(mid[:, s, :, 2, 96:128], dots[:, :, 0, :], dots[:, :, 1, :], ALU.add))
                wait(q)
                nc.vector.tensor_tensor(c4, c4, part[:, 1, :, :, :], ALU.add).then_inc(products_done[s], 1)
                assert r == K, r

            def add(g):
                if g is None:
                    return
                base = win.start_of(dve, g.rnd, g.u)
                dve.wait_ge(mixed[g.s], g.n + 1)
                dve.wait_ge(added, g.k)
                nc.vector.tensor_tensor(core.acc[:, ds(base, WIN)], core.acc[:, ds(base, WIN)],
                                        pw[g.s][:, 0:WIN], ALU.add).then_inc(added, 1)

            with dve.Fori(0, windows) as w:
                def both(g):
                    products(g, w)
                    add(g.near(-2))
                    if g.near(1) is None:
                        add(g.near(-1))
                        add(g)

                edge_loop(sh, dve, w, both)
                dve.wait_ge(added, (w + 1) * sh.groups)
                win.move_on()

        @block.tensor
        def _(pe):
            windows = win.count(pe)

            def sums(g):
                u, s = g.u, g.s
                pe.wait_ge(chain, g.k * K + K)
                pe.wait_ge(rows_used_dve[u], g.t + 1)
                pe.wait_ge(products_done[s], g.n + 1)
                pe.wait_ge(scaled[u], g.t + 1)
                pe.wait_ge(agg_ready[s], g.n)
                for k in range(3):
                    for j in range(J):
                        last = nc.tensor.matmul(ps[s][:, k, :], mid[:, s, j, k, :], hot[:, s, j, :],
                                                start=(j == 0), stop=(j == J - 1))
                last.then_inc(summed[s], 1)

            def mix(g):
                if g is None:
                    return
                s = g.s
                pe.wait_ge(agg_ready[s], g.n + 1)
                old = g.near(-2)
                if old:
                    pe.wait_ge(added, old.k + 1)
                for k in range(3):
                    last = nc.tensor.matmul(pw[s][:, 0:WIN], w_mix[:, k, :], agg[:, s, k, :],
                                            start=(k == 0), stop=(k == 2))
                last.then_inc(mixed[s], 1)

            def both(g):
                sums(g)
                mix(g.near(-1))
                if g.near(1) is None:
                    mix(g)

            with pe.Fori(0, windows) as w:
                edge_loop(sh, pe, w, both)


H = 4
HD = D // H
Q = J * H
HALF = J // 2
STEPS = 2 * H
ROW = D + H


class Attention:

    def __init__(self, nc, ctx, core):
        self.top = ctx.enter_context(nc.sbuf_tensor("top", [H, core.sh.cols], F32))
        self.den = core.h_flat[0:H, :]


def attention_pass(nc, core, w, att, src, e_attr, table, table_t):
    sh = core.sh
    with ExitStack() as ctx:
        sems_of = StageSemaphores(nc, ctx)
        def sb(name, shape, dt=F32):
            return ctx.enter_context(nc.sbuf_tensor(f"{name}_l2", shape, dt))

        def sem(name):
            return sems_of.new(f"{name}_l2")

        def sems(name, n):
            return [sem(f"{name}{i}") for i in range(n)]

        def psum(name, free):
            return ctx.enter_context(nc.psum_tensor(f"{name}_l2", [P, free], F32))

        win = Windows(nc, ctx, sems_of, core, "l2")
        idx = sb("idx", [P, U, J], I32)
        rows = sb("rows", [P, U, J, ROW])
        e64 = sb("e64", [P, U, J * 64])
        ht = sb("ht", [P, U, H])
        rel_s = sb("rel_s", [P, 2, J])
        hot = sb("hot", [P, U, J, WIN])
        hotT = sb("hotT", [WIN, 2, J, P])
        eT = sb("eT", [P, HALF, P])
        score = sb("score", [P, 2, Q])
        resid = sb("resid", [P, Q])
        split = sb("split", [P, 3 * Q], BF16)
        splitT = sb("splitT", [3 * Q, P], BF16)
        junk = sb("junk", [WIN, 2, HALF * P], BF16)
        high_a = sb("high_a", [WIN, 2, H])
        high = sb("high", [WIN, 2, H])
        top_new = sb("top_new", [H, 2, WIN])
        drop = sb("drop", [H, 2, WIN])
        scale = sb("scale", [H, 2, WIN])
        top_n = sb("top_n", [WIN, 2, H])
        diff = sb("diff", [P, 2, Q])
        wrow = sb("wrow", [P, 2, J, ROW])
        sums = sb("sums", [WIN, 2, ROW])
        p_turn = psum("p_turn", 512)
        p_wide = [psum(f"p_wide{i}", HALF * P) for i in range(2)]
        bank_s = psum("bank_s", 512)
        p_score, p_split = bank_s[:, 0:Q], bank_s[0:3 * Q, 256:320].bitcast(BF16)
        bank_t = psum("bank_t", 512)
        p_high, p_topn, p_top = bank_t[0:H, 128:256], bank_t[:, 0:H], bank_t[:, Q:2 * Q]
        p_sum = psum("p_sum", 512)
        p_out = psum("p_out", 512)
        p_num, p_scale, p_den = p_out[:, 0:128], p_out[:, 128:256], p_out[0:H, 256:384]

        idx_loaded = sems("idx_loaded", U)
        rows_loaded = sems("rows_loaded", U)
        e_loaded = sems("e_loaded", U)
        ht_loaded = sems("ht_loaded", U)
        group_begun = sem("group_begun")
        windows_seen, maxima_begun, tops_begun = sem("windows_seen"), sem("maxima_begun"), sem("tops_begun")
        zeroed, rel_copied, hot_ready = sem("zeroed"), sem("rel_copied"), sem("hot_ready")
        added_score, leaked, split_hi, split_rest, split_mid, split_ready = (
            sem("added_score"), sem("leaked"), sem("split_hi"), sem("split_rest"), sem("split_mid"), sem("split_ready"))
        maxed, top_new_ready, drop_ready, top_done = sem("maxed"), sem("top_new_ready"), sem("drop_ready"), sem("top_done")
        diffed, diff_ready = sem("diffed"), sem("diff_ready")
        weighed = sems("weighed", U)
        acc_scaled, den_scaled, den_done, acc_done = sem("acc_scaled"), sem("den_scaled"), sem("den_done"), sem("acc_done")
        turned_a, turned_b, spread_m = sem("turned_a"), sem("turned_b"), sem("spread_m")
        e_turned = sems("e_turned", U)
        scored = sems("scored", U)
        split_turned, spread_s, high_turned, top_turned = sem("split_turned"), sem("spread_s"), sem("high_turned"), sem("top_turned")
        summed, scale_spread, sums_turned = sem("summed"), sem("scale_spread"), sem("sums_turned")
        hotT_a, hotT_b, eT_ready, splitT_ready = sem("hotT_a"), sem("hotT_b"), sem("eT_ready"), sem("splitT_ready")
        scale_ready, top_n_ready, ex_ready, sums_copied = sem("scale_ready"), sem("top_n_ready"), sem("ex_ready"), sem("sums_copied")
        block = ctx.enter_context(nc.Block())

        @block.sync
        def _(sp):
            windows = win.count(sp)
            with sp.Fori(0, windows) as w_:
                win.wait(sp, w_)
                sp.sem_inc(windows_seen, 1)
                with sp.Fori(0, sh.rounds) as rnd:
                    t = w_ * sh.rounds + rnd
                    for u in range(U):
                        at = ds(sp.snap(sh.first_edge(rnd, u)), GROUP)
                        sp.wait_ge(rows_loaded[u], t * (J * DMA))
                        sp.dma_start(idx[:, u, :], src[at].rearrange("(p j) -> p j", j=J)).then_inc(idx_loaded[u], DMA)
                        sp.wait_ge(e_turned[u], t)
                        sp.dma_start(e64[:, u, :], e_attr[at, :].rearrange("(p j) k -> p (j k)", j=J)).then_inc(e_loaded[u], DMA)
                        base = sp.snap(win.start_of(sp, rnd, u))
                        sp.wait_ge(scored[u], t)
                        sp.dma_start(ht[:, u, :], table_t[ds(base, WIN), :]).then_inc(ht_loaded[u], DMA)

        @block.gpsimd
        def _(pool):
            windows = win.count(pool)
            with pool.Fori(0, windows) as w_:
                with pool.Fori(0, sh.rounds) as rnd:
                    t = w_ * sh.rounds + rnd
                    for u in range(U):
                        pool.wait_ge(idx_loaded[u], t * DMA + DMA)
                        pool.wait_ge(weighed[u], t)
                        pool.sem_inc(group_begun, 1)
                        for j in range(J):
                            pool.indirect_dma_start(
                                out=rows[:, u, j, :], out_offset=None, in_=table,
                                in_offset=bass.IndirectOffsetOnAxis(ap=idx[:, u, j:j + 1], axis=0),
                            ).then_inc(rows_loaded[u], DMA)

        @block.vector
        def _(dve):
            nc.vector.memset(att.top[:, :], 0.0)
            nc.vector.memset(att.den[:, :], 0.0).then_inc(zeroed, 1)
            dve.wait_ge(zeroed, 1)
            win.start()
            windows = win.count(dve)

            def hots(g, w_):
                if g is None:
                    return
                u, s = g.u, g.s
                win.wait(dve, w_)
                nc.vector.tensor_copy(rel_s[:, s, :], win.rel[:, ds(g.rnd * U + u, 1), :].rearrange("p a j -> p (a j)")).then_inc(rel_copied, 1)
                dve.wait_ge(rel_copied, g.k + 1)
                old = g.near(-U)
                if old:
                    dve.wait_ge(summed, old.k + 1)
                for j in range(J):
                    last = nc.vector.tensor_scalar(hot[:, u, j, :], core.iota[:, :], rel_s[:, s, j:j + 1], None, ALU.is_equal)
                last.then_inc(hot_ready, 1)

            def scores(g):
                if g is None:
                    return
                u, s = g.u, g.s
                sc = score[:, s, :]
                dve.wait_ge(scored[u], g.t + 1)
                dve.wait_ge(rows_loaded[u], (g.t + 1) * (J * DMA))
                nc.vector.tensor_tensor(sc.rearrange("p (j h) -> p j h", h=H), rows[:, u, :, D:ROW],
                                        p_score.rearrange("p (j h) -> p j h", h=H), ALU.add).then_inc(added_score, 1)
                dve.wait_ge(added_score, g.k + 1)
                nc.vector.scalar_tensor_tensor(sc, sc, 0.2, sc, ALU.mult, ALU.max).then_inc(leaked, 1)
                dve.wait_ge(leaked, g.k + 1)
                old = g.near(-1)
                if old:
                    dve.wait_ge(split_turned, old.k + 1)
                nc.vector.tensor_copy(split[:, 0:Q], sc).then_inc(split_hi, 1)
                dve.wait_ge(split_hi, g.k + 1)
                nc.vector.tensor_tensor(resid[:, :], sc, split[:, 0:Q], ALU.subtract).then_inc(split_rest, 1)
                dve.wait_ge(split_rest, g.k + 1)
                nc.vector.tensor_copy(split[:, Q:2 * Q], resid[:, :]).then_inc(split_mid, 1)
                dve.wait_ge(split_mid, g.k + 1)
                nc.vector.tensor_tensor(split[:, 2 * Q:3 * Q], resid[:, :], split[:, Q:2 * Q], ALU.subtract).then_inc(split_ready, 1)

            def maxima(g):
                s = g.s
                dve.wait_ge(hotT_b, g.k + 1)
                for i in range(STEPS):
                    half, h = divmod(i, H)
                    dve.wait_ge(spread_s, g.k * STEPS + i + 1)
                    old = g.near(-1)
                    if i >= 2 or old:
                        dve.wait_ge(maxed, g.k * STEPS + i - 1 if i >= 2 else old.k * STEPS + i + STEPS - 1)
                    dve.sem_inc(maxima_begun, 1)
                    nc.vector.tensor_tensor_reduce(
                        out=junk[:, i % 2, :], in0=p_wide[i % 2][:, :],
                        in1=hotT[:, s, half * HALF:(half + 1) * HALF, :].rearrange("p j e -> p (j e)"),
                        scale=1.0, scalar=high_a[:, s, h:h + 1] if half else 0.0, op0=ALU.mult, op1=ALU.max,
                        accum_out=(high if half else high_a)[:, s, h:h + 1]).then_inc(maxed, 1)

            def new_tops(g):
                s = g.s
                base = win.start_of(dve, g.rnd, g.u)
                old = att.top[:, ds(base, WIN)]
                dve.wait_ge(high_turned, g.k + 1)
                dve.wait_ge(top_done, g.k)
                nc.vector.tensor_tensor(top_new[:, s, :], old, p_high, ALU.max).then_inc(top_new_ready, 1)
                dve.wait_ge(top_new_ready, g.k + 1)
                nc.vector.tensor_tensor(drop[:, s, :], old, top_new[:, s, :], ALU.subtract).then_inc(drop_ready, 1)
                return old

            def keep_tops(g, old):
                dve.wait_ge(drop_ready, g.k + 1)
                nc.vector.tensor_scalar(old, top_new[:, g.s, :], 0.0, None, ALU.max).then_inc(top_done, 1)

            def add(g):
                if g is None:
                    return
                s = g.s
                base = win.start_of(dve, g.rnd, g.u)
                acc, den = core.acc[:, ds(base, WIN)], att.den[:, ds(base, WIN)]
                dve.wait_ge(sums_turned, g.k + 1)
                dve.wait_ge(acc_done, g.k)
                nc.vector.tensor_tensor(acc, acc, p_scale, ALU.mult).then_inc(acc_scaled, 1)
                nc.vector.tensor_tensor(den, den, scale[:, s, :], ALU.mult).then_inc(den_scaled, 1)
                dve.wait_ge(den_scaled, g.k + 1)
                nc.vector.tensor_tensor(den, den, p_den, ALU.add).then_inc(den_done, 1)
                nc.vector.tensor_tensor(acc, acc, p_num, ALU.add).then_inc(acc_done, 1)

            def differences(g):
                s = g.s
                dve.wait_ge(spread_m, g.k + 1)
                nc.vector.tensor_tensor(diff[:, s, :], score[:, s, :], p_top, ALU.subtract).then_inc(diffed, 1)
                dve.wait_ge(diffed, g.k + 1)
                nc.vector.tensor_scalar(diff[:, s, :], diff[:, s, :], 0.0, None, ALU.min).then_inc(diff_ready, 1)

            def weigh(g):
                u, s = g.u, g.s
                dve.wait_ge(ex_ready, g.k + 1)
                wide = [P, J, H, HD]
                nc.vector.tensor_tensor(wrow[:, s, :, 0:D].rearrange("p j (h c) -> p j h c", h=H),
                                        rows[:, u, :, 0:D].rearrange("p j (h c) -> p j h c", h=H),
                                        wrow[:, s, :, D:ROW].unsqueeze(3).broadcast_to(wide), ALU.mult).then_inc(weighed[u], 1)

            with dve.Fori(0, windows) as w_:
                def body(g):
                    if g.near(-1) is None:
                        hots(g, w_)
                        hots(g.near(1), w_)
                        scores(g)
                    maxima(g)
                    scores(g.near(1))
                    old = new_tops(g)
                    add(g.near(-1))
                    keep_tops(g, old)
                    differences(g)
                    hots(g.near(2), w_)
                    weigh(g)
                    if g.near(1) is None:
                        add(g)

                edge_loop(sh, dve, w_, body)
                dve.wait_ge(acc_done, (w_ + 1) * sh.groups)
                win.move_on()

        @block.tensor
        def _(pe):
            windows = win.count(pe)

            def turn_hots(g, half):
                if g is None:
                    return
                if half == 0:
                    pe.wait_ge(hot_ready, g.k + 1)
                    old = g.near(-1)
                    if old:
                        pe.wait_ge(eT_ready, old.k + 1)
                else:
                    pe.wait_ge(hotT_a, g.k + 1)
                for j in range(HALF):
                    last = nc.tensor.transpose(p_turn[:, j * P:(j + 1) * P], hot[:, g.u, half * HALF + j, :], core.ident[:, :])
                last.then_inc(turned_b if half else turned_a, 1)

            def turn_edges(g):
                if g is None:
                    return
                u = g.u
                pe.wait_ge(e_loaded[u], g.t * DMA + DMA)
                pe.wait_ge(hotT_b, g.k + 1)
                for j in range(HALF):
                    last = nc.tensor.transpose(p_turn[:, j * P:(j + 1) * P], e64[:, u, j * P:(j + 1) * P], core.ident[:, :])
                last.then_inc(e_turned[u], 1)

            def score(g):
                if g is None:
                    return
                u, s = g.u, g.s
                pe.wait_ge(eT_ready, g.k + 1)
                pe.wait_ge(ht_loaded[u], g.t * DMA + DMA)
                old = g.near(-1)
                if old:
                    pe.wait_ge(splitT_ready, old.k + 1)
                for j in range(HALF):
                    nc.tensor.matmul(p_score[:, 2 * H * j:2 * H * (j + 1)], eT[:, j, :], w.edge[:, :],
                                     start=(j == 0), stop=False, skip_group_check=True)
                for j in range(J):
                    last = nc.tensor.matmul(p_score[:, H * j:H * (j + 1)], hotT[:, s, j, :], ht[:, u, :],
                                            start=False, stop=(j == J - 1), skip_group_check=True)
                last.then_inc(scored[u], 1)

            def turn_split(g):
                if g is None:
                    return
                pe.wait_ge(split_ready, g.k + 1)
                nc.tensor.transpose(p_split, split[:, :], w.ident_b[:, :]).then_inc(split_turned, 1)

            def spread_scores(g, first, last_):
                for i in range(first, last_):
                    half, h = divmod(i, H)
                    if i == 0:
                        pe.wait_ge(splitT_ready, g.k + 1)
                    old = g.near(-1)
                    if i >= 2 or old:
                        pe.wait_ge(maxed, g.k * STEPS + i - 1 if i >= 2 else old.k * STEPS + i + STEPS - 1)
                    for j in range(HALF):
                        last = nc.tensor.matmul(p_wide[i % 2][:, j * P:(j + 1) * P],
                                                w.pick[:, H * (half * HALF + j) + h, :], splitT[:, :],
                                                start=True, stop=True)
                    last.then_inc(spread_s, 1)

            def tops(g):
                s = g.s
                pe.wait_ge(top_new_ready, g.k + 1)
                pe.sem_inc(tops_begun, 1)
                nc.tensor.transpose(p_topn, top_new[:, s, :], core.ident[0:H, 0:H]).then_inc(top_turned, 1)
                pe.wait_ge(top_n_ready, g.k + 1)
                for j in range(J):
                    last = nc.tensor.matmul(p_top[:, H * j:H * (j + 1)], hotT[:, s, j, :], top_n[:, s, :],
                                            start=(j == 0), stop=(j == J - 1), skip_group_check=True)
                last.then_inc(spread_m, 1)

            def out(g):
                u, s = g.u, g.s
                pe.wait_ge(scale_ready, g.k + 1)
                pe.wait_ge(acc_done, g.k)
                nc.tensor.matmul(p_scale, w.heads[:, :], scale[:, s, :], start=True, stop=True).then_inc(scale_spread, 1)
                pe.wait_ge(weighed[u], g.t + 1)
                pe.wait_ge(sums_copied, g.k)
                for j in range(J):
                    last = nc.tensor.matmul(p_sum[:, 0:ROW], hot[:, u, j, :], wrow[:, s, j, :],
                                            start=(j == 0), stop=(j == J - 1))
                last.then_inc(summed, 1)

            def turn_sums(g):
                s = g.s
                pe.wait_ge(sums_copied, g.k + 1)
                nc.tensor.transpose(p_num, sums[:, s, 0:D], core.ident[:, :])
                nc.tensor.transpose(p_den, sums[:, s, D:ROW], core.ident[:, :]).then_inc(sums_turned, 1)

            with pe.Fori(0, windows) as w_:
                def body(g):
                    nxt = g.near(1)
                    if g.near(-1) is None:
                        turn_hots(g, 0)
                        turn_hots(g, 1)
                        turn_edges(g)
                        score(g)
                        turn_split(g)
                    spread_scores(g, 0, 2)
                    turn_hots(nxt, 0)
                    spread_scores(g, 2, 4)
                    turn_hots(nxt, 1)
                    spread_scores(g, 4, 6)
                    turn_edges(nxt)
                    spread_scores(g, 6, STEPS)
                    score(nxt)
                    pe.wait_ge(maxed, (g.k + 1) * STEPS)
                    old = g.near(-1)
                    if old:
                        pe.wait_ge(diffed, old.k + 1)
                    nc.tensor.transpose(p_high, high[:, g.s, :], core.ident[:, :]).then_inc(high_turned, 1)
                    turn_split(nxt)
                    tops(g)
                    out(g)
                    turn_sums(g)

                edge_loop(sh, pe, w_, body)

        @block.scalar
        def _(act):
            windows = win.count(act)

            def turned(g):
                if g is None:
                    return
                s = g.s
                act.wait_ge(turned_a, g.k + 1)
                old = g.near(-2)
                if old:
                    act.wait_ge(spread_m, old.k + 1)
                nc.scalar.copy(hotT[:, s, 0:HALF, :], p_turn[:, :].rearrange("p (j e) -> p j e", e=P)).then_inc(hotT_a, 1)
                act.wait_ge(turned_b, g.k + 1)
                nc.scalar.copy(hotT[:, s, HALF:J, :], p_turn[:, :].rearrange("p (j e) -> p j e", e=P)).then_inc(hotT_b, 1)
                act.wait_ge(e_turned[g.u], g.t + 1)
                old = g.near(-1)
                if old:
                    act.wait_ge(scored[old.u], old.t + 1)
                nc.scalar.copy(eT[:, :, :], p_turn[:, :].rearrange("p (j e) -> p j e", e=P)).then_inc(eT_ready, 1)

            def split_scores(g):
                if g is None:
                    return
                act.wait_ge(split_turned, g.k + 1)
                old = g.near(-1)
                if old:
                    act.wait_ge(spread_s, (old.k + 1) * STEPS)
                nc.scalar.copy(splitT[:, :], p_split).then_inc(splitT_ready, 1)

            with act.Fori(0, windows) as w_:
                def body(g):
                    nxt, s = g.near(1), g.s
                    if g.near(-1) is None:
                        turned(g)
                        split_scores(g)
                    turned(nxt)
                    split_scores(nxt)
                    act.wait_ge(top_turned, g.k + 1)
                    nc.scalar.copy(top_n[:, s, :], p_topn).then_inc(top_n_ready, 1)
                    act.wait_ge(drop_ready, g.k + 1)
                    nc.scalar.activation(scale[:, s, :], drop[:, s, :], ACT.Exp).then_inc(scale_ready, 1)
                    act.wait_ge(diff_ready, g.k + 1)
                    old = g.near(-2)
                    if old:
                        act.wait_ge(summed, old.k + 1)
                    nc.scalar.activation(wrow[:, s, :, D:ROW], diff[:, s, :].rearrange("p (j h) -> p j h", h=H), ACT.Exp).then_inc(ex_ready, 1)
                    act.wait_ge(summed, g.k + 1)
                    nc.scalar.copy(sums[:, s, :], p_sum[:, 0:ROW]).then_inc(sums_copied, 1)

                edge_loop(sh, act, w_, body)


LAST = 4


def build(nc, a, out):
    sh = Shapes(a["x"].shape[0], a["src"].shape[0])
    table0 = nc.dram_tensor("table0", (sh.rows, D), F32, kind="Internal").ap()
    table1 = nc.dram_tensor("table1", (sh.rows, D), F32, kind="Internal").ap()
    table2 = nc.dram_tensor("table2", (sh.rows, 132), F32, kind="Internal").ap()
    table2_t = nc.dram_tensor("table2_t", (sh.cols, 4), F32, kind="Internal").ap()
    table3 = nc.dram_tensor("table3", (sh.rows, D), F32, kind="Internal").ap()
    with ExitStack() as ctx:
        core = Core(nc, ctx, sh)
        w = Weights(nc, ctx)
        setup_stage(nc, core, a["x"], a["dst"])
        weights_stage(nc, core, w, a)
        degree_stage(nc, core)
        node_stage(nc, core, 0, table0)
        sum_pass(nc, core, a["src"], table0, "l0")
        node_stage(nc, core, 1, table1)
        if LAST >= 2:
            tensor_pass(nc, core, w.mix, a["src"], a["edge_attr_9"], table1)
            node_stage(nc, core, 2, table2, table2_t, w=w)
        if LAST >= 3:
            att = Attention(nc, ctx, core)
            attention_pass(nc, core, w, att, a["src"], a["edge_attr_64"], table2, table2_t)
            node_stage(nc, core, 3, table3, att=att)
        if LAST >= 4:
            sum_pass(nc, core, a["src"], table3, "l3")
            node_stage(nc, core, 4, out=out, w=w)
            return
        dump(nc, core, out)


def dump(nc, core, out):
    sh = core.sh
    with ExitStack() as ctx:
        done = ctx.enter_context(nc.semaphore("done"))
        block = ctx.enter_context(nc.Block())
        full = (sh.blocks - 1) * P

        @block.sync
        def _(sp):
            sp.dma_start(out[0:full, :].rearrange("(b p) d -> p b d", p=P), core.x[:, 0:sh.blocks - 1, :]).then_inc(done, DMA)
            sp.dma_start(out[full:sh.n, :], core.x[0:sh.last_block, sh.blocks - 1, :]).then_inc(done, DMA)
            sp.wait_ge(done, 2 * DMA)


_INS = ["x", "src", "dst", "edge_attr_64", "edge_attr_9", "L1_gnn_w0", "L1_gnn_w1", "L1_gnn_w2", "L1_gnn_w3",
        "L1_gnn_w4", "L2_gnn_W_node", "L2_gnn_W_edge", "L2_gnn_a", "L3_gnn_W_self", "L3_gnn_b_self",
        "L3_gnn_W_msg", "L3_gnn_b_msg", "L3_gnn_ln_gamma", "L3_gnn_ln_beta"]


def kernel(**inputs):
    import numpy as _np
    import concourse.bacc as _bacc
    from concourse import mybir as _mybir
    from concourse.bass_utils import run_bass_kernel_spmd as _run

    nc = _bacc.Bacc("TRN2", target_bir_lowering=False, num_devices=1)
    arrays, args = {}, {}
    for name in _INS:
        arr = _np.ascontiguousarray(inputs[name])
        arrays[f"in_{name}"] = arr
        args[name] = nc.dram_tensor(f"in_{name}", arr.shape, _mybir.dt.from_np(arr.dtype), kind="ExternalInput").ap()
    out = nc.dram_tensor("out_0", inputs["x"].shape, _mybir.dt.float32, kind="ExternalOutput").ap()
    build(nc, args, out)
    r = _run(nc, [arrays], core_ids=[0])
    return r.results[0]["out_0"]
```
